# Optimizing a Trainium2 kernel written in Bass

```python
import numpy as np
import jax
import jax.numpy as jnp

def _softmax(x, axis=-1):
    return jax.nn.softmax(x, axis=axis)

def _gelu(x):
    return jax.nn.gelu(x, approximate=True)

def _silu(x):
    return jax.nn.silu(x)

def _sigmoid(x):
    return jax.nn.sigmoid(x)

def _layernorm(x, axis=-1, eps=1e-05):
    m = jnp.mean(x, axis=axis, keepdims=True)
    v = jnp.var(x, axis=axis, keepdims=True)
    return (x - m) / jnp.sqrt(v + eps)

def _scatter_add(tgt, idx, src, axis=0):
    return tgt.at[idx].add(src)

def _segment_sum(src, seg, n):
    return jax.ops.segment_sum(src, seg, n)
kernel_name = 'mk_audio_tower_d1_tok_aud1d768_r4_f2a7bf'

def setup_inputs(seed: int=0):
    np.random.seed(seed)
    _w = jnp.asarray

    def _rec_inputs():
        import jax
        import jax.numpy as jnp
        _rk = jax.random.key(seed)
        x = -6.41493e-05 + 1.00002 * jax.random.normal(jax.random.fold_in(_rk, 1), (16, 120000), jnp.float32)
        return x
    x = _rec_inputs()

    def _L0_tok_setup():
        import jax, jax.numpy as jnp
        import numpy as np
        import math
        SR = 4000
        FRAME_LEN = 100
        FRAME_STEP = 160
        N_FILTERS = 40
        N_MFCC = 13
        EMBED = 192
        BATCH = 64
        AUDIO_LEN = 40000
        N_FFT_BINS = FRAME_LEN // 2 + 1

        def _mel_filterbank():
            low_mel = 2595.0 * math.log10(1.0 + 0.0 / 700.0)
            high_mel = 2595.0 * math.log10(1.0 + SR // 2 / 700.0)
            mel_points = np.linspace(low_mel, high_mel, N_FILTERS + 2)
            hz_points = 700.0 * (10.0 ** (mel_points / 2595.0) - 1.0)
            bin_points = np.floor((FRAME_LEN + 1) * hz_points / SR)
            filt = np.zeros((N_FILTERS, N_FFT_BINS), dtype=np.float32)
            for i in range(1, N_FILTERS + 1):
                l, c, r = (bin_points[i - 1], bin_points[i], bin_points[i + 1])
                for j in range(int(l), int(c)):
                    filt[i - 1, j] = (j - l) / (c - l)
                for j in range(int(c), int(r)):
                    filt[i - 1, j] = (r - j) / (r - c)
            return jnp.asarray(filt)

        def _dct_matrix():
            k = np.arange(N_MFCC)[:, None]
            j = np.arange(N_FILTERS)[None, :]
            m = np.cos(np.pi * k * (2 * j + 1) / (2 * N_FILTERS)) * math.sqrt(2.0 / N_FILTERS)
            return jnp.asarray(m.astype(np.float32))
        key = jax.random.key(seed)
        kx, kw = jax.random.split(key)
        x = jax.random.normal(kx, (BATCH, AUDIO_LEN), dtype=jnp.float32)
        bound = 1.0 / math.sqrt(N_MFCC)
        w_proj = jax.random.uniform(kw, (N_MFCC, EMBED), minval=-bound, maxval=bound, dtype=jnp.float32)
        b_proj = jnp.zeros((EMBED,), dtype=jnp.float32)
        return {'x': x, 'mel_filters': _mel_filterbank(), 'dct': _dct_matrix(), 'w_proj': w_proj, 'b_proj': b_proj}
    _L0_tok_all = _L0_tok_setup()
    _L0_tok_in = {k: v for k, v in _L0_tok_all.items() if k in ('mel_filters', 'dct', 'w_proj', 'b_proj')}
    del _L0_tok_all

    def _L0_attn_setup():
        import jax, jax.numpy as jnp
        import numpy as np
        NUM_HEADS = 12

        def _split_heads(x, N, S):
            return x.reshape(N, S, NUM_HEADS, -1).transpose(0, 2, 1, 3)
        key = jax.random.key(seed)
        ks = jax.random.split(key, 12)
        N, S, E, R, RM = (8, 256, 192, 96, 64)
        hd = E // NUM_HEADS
        s = 0.02
        return {'hidden_states': jax.random.normal(ks[0], (N, S, E), dtype=jnp.float32), 'U_Q': jax.random.normal(ks[1], (R, E), dtype=jnp.float32) * s, 'V_Q': jax.random.normal(ks[2], (E, R), dtype=jnp.float32) * s, 'U_K': jax.random.normal(ks[3], (R, E), dtype=jnp.float32) * s, 'V_K': jax.random.normal(ks[4], (E, R), dtype=jnp.float32) * s, 'U_V': jax.random.normal(ks[5], (R, E), dtype=jnp.float32) * s, 'V_V': jax.random.normal(ks[6], (E, R), dtype=jnp.float32) * s, 'bias_q': jax.random.normal(ks[7], (E,), dtype=jnp.float32) * s, 'bias_k': jax.random.normal(ks[8], (E,), dtype=jnp.float32) * s, 'bias_v': jax.random.normal(ks[9], (E,), dtype=jnp.float32) * s, 'M_U': jax.random.normal(ks[10], (hd, RM), dtype=jnp.float32) * 0.1, 'M_V': jax.random.normal(ks[11], (RM, hd), dtype=jnp.float32) * 0.1}
    _L0_attn_all = _L0_attn_setup()
    _L0_attn_in = {k: v for k, v in _L0_attn_all.items() if k in ('U_Q', 'V_Q', 'U_K', 'V_K', 'U_V', 'V_V', 'bias_q', 'bias_k', 'bias_v', 'M_U', 'M_V')}
    del _L0_attn_all

    def _L0_ffn_setup():
        import jax, jax.numpy as jnp
        import numpy as np
        B, S, D = (2, 256, 192)
        I = 96
        E = 8
        G = 4
        TOPK_GROUPS = 2
        K = 2
        ROUTE_SCALE = 1.0
        ALPHA, LIMIT = (1.702, 7.0)

        def swiglu(h):
            xg = jnp.minimum(h[..., ::2], LIMIT)
            xl = jnp.clip(h[..., 1::2], -LIMIT, LIMIT)
            return xg * jax.nn.sigmoid(ALPHA * xg) * (xl + 1.0)

        def gate(x, gate_w, gate_b):
            scores = jax.nn.softmax(jnp.einsum('td,ed->te', x, gate_w).astype(jnp.float32), axis=-1)
            original_scores = scores
            s = scores + gate_b
            T = x.shape[0]
            sg = s.reshape(T, G, E // G)
            group_scores = jnp.sum(jax.lax.top_k(sg, 2)[0], axis=-1)
            _, gidx = jax.lax.top_k(group_scores, TOPK_GROUPS)
            keep = jnp.any(jax.nn.one_hot(gidx, G, dtype=jnp.bool_), axis=1)
            sg = jnp.where(keep[:, :, None], sg, -jnp.inf)
            s = sg.reshape(T, E)
            _, idx = jax.lax.top_k(s, K)
            w = jnp.take_along_axis(original_scores, idx, axis=1) * ROUTE_SCALE
            return (w.astype(x.dtype), idx)

        def expert_ffn(x, W1, B1, W3, B3, W2, B2):
            h1 = jnp.einsum('td,edh->teh', x, W1) + B1
            h3 = jnp.einsum('td,edh->teh', x, W3) + B3
            g = swiglu(h1 * h3)
            return jnp.einsum('tei,eid->ted', g, W2) + B2

        def shared_ffn(x, Ws1, Bs1, Ws3, Bs3, Ws2, Bs2):
            h = (x @ Ws1 + Bs1) * (x @ Ws3 + Bs3)
            return swiglu(h) @ Ws2 + Bs2
        key = jax.random.key(seed)
        ks = jax.random.split(key, 16)
        sc = 0.02
        inp = {'x': jax.random.normal(ks[0], (B, S, D), jnp.float32), 'gate_w': jax.random.normal(ks[1], (E, D), jnp.float32) * sc, 'gate_b': jax.random.normal(ks[2], (E,), jnp.float32) * sc, 'W1': jax.random.normal(ks[3], (E, D, 2 * I), jnp.float32) * sc, 'B1': jax.random.normal(ks[4], (E, 2 * I), jnp.float32) * sc, 'W3': jax.random.normal(ks[5], (E, D, 2 * I), jnp.float32) * sc, 'B3': jax.random.normal(ks[6], (E, 2 * I), jnp.float32) * sc, 'W2': jax.random.normal(ks[7], (E, I, D), jnp.float32) * sc, 'B2': jax.random.normal(ks[8], (E, D), jnp.float32) * sc, 'Ws1': jax.random.normal(ks[9], (D, 2 * I), jnp.float32) * sc, 'Bs1': jax.random.normal(ks[10], (2 * I,), jnp.float32) * sc, 'Ws3': jax.random.normal(ks[11], (D, 2 * I), jnp.float32) * sc, 'Bs3': jax.random.normal(ks[12], (2 * I,), jnp.float32) * sc, 'Ws2': jax.random.normal(ks[13], (I, D), jnp.float32) * sc, 'Bs2': jax.random.normal(ks[14], (D,), jnp.float32) * sc}
        return inp
    _L0_ffn_all = _L0_ffn_setup()
    _L0_ffn_in = {k: v for k, v in _L0_ffn_all.items() if k in ('gate_w', 'gate_b', 'W1', 'B1', 'W3', 'B3', 'W2', 'B2', 'Ws1', 'Bs1', 'Ws3', 'Bs3', 'Ws2', 'Bs2')}
    del _L0_ffn_all
    return {'x': x, 'L0_tok_mel_filters': _L0_tok_in['mel_filters'], 'L0_tok_dct': _L0_tok_in['dct'], 'L0_tok_w_proj': _L0_tok_in['w_proj'], 'L0_tok_b_proj': _L0_tok_in['b_proj'], 'L0_attn_U_Q': _L0_attn_in['U_Q'], 'L0_attn_V_Q': _L0_attn_in['V_Q'], 'L0_attn_U_K': _L0_attn_in['U_K'], 'L0_attn_V_K': _L0_attn_in['V_K'], 'L0_attn_U_V': _L0_attn_in['U_V'], 'L0_attn_V_V': _L0_attn_in['V_V'], 'L0_attn_bias_q': _L0_attn_in['bias_q'], 'L0_attn_bias_k': _L0_attn_in['bias_k'], 'L0_attn_bias_v': _L0_attn_in['bias_v'], 'L0_attn_M_U': _L0_attn_in['M_U'], 'L0_attn_M_V': _L0_attn_in['M_V'], 'L0_ffn_gate_w': _L0_ffn_in['gate_w'], 'L0_ffn_gate_b': _L0_ffn_in['gate_b'], 'L0_ffn_W1': _L0_ffn_in['W1'], 'L0_ffn_B1': _L0_ffn_in['B1'], 'L0_ffn_W3': _L0_ffn_in['W3'], 'L0_ffn_B3': _L0_ffn_in['B3'], 'L0_ffn_W2': _L0_ffn_in['W2'], 'L0_ffn_B2': _L0_ffn_in['B2'], 'L0_ffn_Ws1': _L0_ffn_in['Ws1'], 'L0_ffn_Bs1': _L0_ffn_in['Bs1'], 'L0_ffn_Ws3': _L0_ffn_in['Ws3'], 'L0_ffn_Bs3': _L0_ffn_in['Bs3'], 'L0_ffn_Ws2': _L0_ffn_in['Ws2'], 'L0_ffn_Bs2': _L0_ffn_in['Bs2']}

def reference(x, L0_tok_mel_filters, L0_tok_dct, L0_tok_w_proj, L0_tok_b_proj, L0_attn_U_Q, L0_attn_V_Q, L0_attn_U_K, L0_attn_V_K, L0_attn_U_V, L0_attn_V_V, L0_attn_bias_q, L0_attn_bias_k, L0_attn_bias_v, L0_attn_M_U, L0_attn_M_V, L0_ffn_gate_w, L0_ffn_gate_b, L0_ffn_W1, L0_ffn_B1, L0_ffn_W3, L0_ffn_B3, L0_ffn_W2, L0_ffn_B2, L0_ffn_Ws1, L0_ffn_Bs1, L0_ffn_Ws3, L0_ffn_Bs3, L0_ffn_Ws2, L0_ffn_Bs2):
    import jax
    import jax.numpy as jnp

    def _L0_tok_ref(x, mel_filters, dct, w_proj, b_proj):
        import jax, jax.numpy as jnp
        import numpy as np
        import math
        SR = 4000
        FRAME_LEN = 100
        FRAME_STEP = 160
        N_FILTERS = 40
        N_MFCC = 13
        EMBED = 192
        BATCH = 64
        AUDIO_LEN = 40000
        N_FFT_BINS = FRAME_LEN // 2 + 1

        def _mel_filterbank():
            low_mel = 2595.0 * math.log10(1.0 + 0.0 / 700.0)
            high_mel = 2595.0 * math.log10(1.0 + SR // 2 / 700.0)
            mel_points = np.linspace(low_mel, high_mel, N_FILTERS + 2)
            hz_points = 700.0 * (10.0 ** (mel_points / 2595.0) - 1.0)
            bin_points = np.floor((FRAME_LEN + 1) * hz_points / SR)
            filt = np.zeros((N_FILTERS, N_FFT_BINS), dtype=np.float32)
            for i in range(1, N_FILTERS + 1):
                l, c, r = (bin_points[i - 1], bin_points[i], bin_points[i + 1])
                for j in range(int(l), int(c)):
                    filt[i - 1, j] = (j - l) / (c - l)
                for j in range(int(c), int(r)):
                    filt[i - 1, j] = (r - j) / (r - c)
            return jnp.asarray(filt)

        def _dct_matrix():
            k = np.arange(N_MFCC)[:, None]
            j = np.arange(N_FILTERS)[None, :]
            m = np.cos(np.pi * k * (2 * j + 1) / (2 * N_FILTERS)) * math.sqrt(2.0 / N_FILTERS)
            return jnp.asarray(m.astype(np.float32))
        B, T = x.shape
        n_frames = 1 + (T - FRAME_LEN) // FRAME_STEP
        idx = jnp.arange(n_frames)[:, None] * FRAME_STEP + jnp.arange(FRAME_LEN)[None, :]
        frames = x[:, idx]
        window = 0.54 - 0.46 * jnp.cos(2.0 * jnp.pi * jnp.arange(FRAME_LEN, dtype=jnp.float32) / (FRAME_LEN - 1))
        windowed = frames * window
        fft = jnp.fft.rfft(windowed, axis=-1)
        power = fft.real ** 2 + fft.imag ** 2
        mel_energies = jnp.einsum('bnf,mf->bnm', power, mel_filters)
        log_energies = jnp.log(mel_energies + 1e-06)
        mfcc = jnp.einsum('bnm,km->bnk', log_energies, dct)
        out = mfcc @ w_proj + b_proj
        return out

    def _L0_attn_ref(hidden_states, U_Q, V_Q, U_K, V_K, U_V, V_V, bias_q, bias_k, bias_v, M_U, M_V):
        import jax, jax.numpy as jnp
        import numpy as np
        NUM_HEADS = 12

        def _split_heads(x, N, S):
            return x.reshape(N, S, NUM_HEADS, -1).transpose(0, 2, 1, 3)
        N, S, E = hidden_states.shape
        hd = E // NUM_HEADS
        scale = 1.0 / jnp.sqrt(jnp.asarray(hd, hidden_states.dtype))
        q = hidden_states @ V_Q @ U_Q + bias_q
        k = hidden_states @ V_K @ U_K + bias_k
        v = hidden_states @ V_V @ U_V + bias_v
        q = _split_heads(q, N, S)
        k = _split_heads(k, N, S)
        v = _split_heads(v, N, S)
        qm = jnp.einsum('bhsd,dr->bhsr', q, M_U)
        km = jnp.einsum('rd,bhtd->bhrt', M_V, k)
        attn = jnp.einsum('bhsr,bhrt->bhst', qm, km) * scale
        attn = jax.nn.softmax(attn, axis=-1)
        out = jnp.einsum('bhst,bhtd->bhsd', attn, v)
        out = out.transpose(0, 2, 1, 3).reshape(N, S, E)
        return out

    def _L0_ffn_ref(x, gate_w, gate_b, W1, B1, W3, B3, W2, B2, Ws1, Bs1, Ws3, Bs3, Ws2, Bs2):
        import jax, jax.numpy as jnp
        import numpy as np
        B, S, D = (2, 256, 192)
        I = 96
        E = 8
        G = 4
        TOPK_GROUPS = 2
        K = 2
        ROUTE_SCALE = 1.0
        ALPHA, LIMIT = (1.702, 7.0)

        def swiglu(h):
            xg = jnp.minimum(h[..., ::2], LIMIT)
            xl = jnp.clip(h[..., 1::2], -LIMIT, LIMIT)
            return xg * jax.nn.sigmoid(ALPHA * xg) * (xl + 1.0)

        def gate(x, gate_w, gate_b):
            scores = jax.nn.softmax(jnp.einsum('td,ed->te', x, gate_w).astype(jnp.float32), axis=-1)
            original_scores = scores
            s = scores + gate_b
            T = x.shape[0]
            sg = s.reshape(T, G, E // G)
            group_scores = jnp.sum(jax.lax.top_k(sg, 2)[0], axis=-1)
            _, gidx = jax.lax.top_k(group_scores, TOPK_GROUPS)
            keep = jnp.any(jax.nn.one_hot(gidx, G, dtype=jnp.bool_), axis=1)
            sg = jnp.where(keep[:, :, None], sg, -jnp.inf)
            s = sg.reshape(T, E)
            _, idx = jax.lax.top_k(s, K)
            w = jnp.take_along_axis(original_scores, idx, axis=1) * ROUTE_SCALE
            return (w.astype(x.dtype), idx)

        def expert_ffn(x, W1, B1, W3, B3, W2, B2):
            h1 = jnp.einsum('td,edh->teh', x, W1) + B1
            h3 = jnp.einsum('td,edh->teh', x, W3) + B3
            g = swiglu(h1 * h3)
            return jnp.einsum('tei,eid->ted', g, W2) + B2

        def shared_ffn(x, Ws1, Bs1, Ws3, Bs3, Ws2, Bs2):
            h = (x @ Ws1 + Bs1) * (x @ Ws3 + Bs3)
            return swiglu(h) @ Ws2 + Bs2
        inp_shape = x.shape
        xt = x.reshape(-1, D)
        w, idx = gate(xt, gate_w, gate_b)
        combine = jnp.einsum('tk,tke->te', w, jax.nn.one_hot(idx, E, dtype=w.dtype))
        per_expert = expert_ffn(xt, W1, B1, W3, B3, W2, B2)
        routed = jnp.einsum('ted,te->td', per_expert, combine)
        out = routed + shared_ffn(xt, Ws1, Bs1, Ws3, Bs3, Ws2, Bs2)
        return out.reshape(inp_shape)
    h = _L0_tok_ref(x, L0_tok_mel_filters, L0_tok_dct, L0_tok_w_proj, L0_tok_b_proj)
    h = h + _L0_attn_ref(_layernorm(h, axis=-1), L0_attn_U_Q, L0_attn_V_Q, L0_attn_U_K, L0_attn_V_K, L0_attn_U_V, L0_attn_V_V, L0_attn_bias_q, L0_attn_bias_k, L0_attn_bias_v, L0_attn_M_U, L0_attn_M_V)
    h = h + _L0_ffn_ref(_layernorm(h, axis=-1), L0_ffn_gate_w, L0_ffn_gate_b, L0_ffn_W1, L0_ffn_B1, L0_ffn_W3, L0_ffn_B3, L0_ffn_W2, L0_ffn_B2, L0_ffn_Ws1, L0_ffn_Bs1, L0_ffn_Ws3, L0_ffn_Bs3, L0_ffn_Ws2, L0_ffn_Bs2)
    return h

_drawn_inputs = setup_inputs


def setup_inputs(seed=0):
    import zlib

    import numpy as np

    out = dict(_drawn_inputs(seed))
    spreads = {'L0_tok_b_proj': (0.0, 0.333)}
    factors = {'L0_attn_U_Q': 8.0,
     'L0_attn_V_Q': 8.0,
     'L0_attn_U_K': 8.0,
     'L0_attn_V_K': 8.0,
     'L0_attn_U_V': 4.494,
     'L0_attn_V_V': 4.145,
     'L0_attn_bias_q': 8.0,
     'L0_attn_bias_v': 8.0,
     'L0_attn_M_U': 8.0,
     'L0_attn_M_V': 8.0,
     'L0_ffn_gate_w': 8.0,
     'L0_ffn_gate_b': 200.0,
     'L0_ffn_W1': 8.0,
     'L0_ffn_B1': 8.0,
     'L0_ffn_W3': 8.0,
     'L0_ffn_B3': 8.0,
     'L0_ffn_W2': 8.0,
     'L0_ffn_B2': 59.602,
     'L0_ffn_Ws1': 8.0,
     'L0_ffn_Bs1': 8.0,
     'L0_ffn_Ws3': 8.0,
     'L0_ffn_Bs3': 8.0,
     'L0_ffn_Ws2': 8.0,
     'L0_ffn_Bs2': 59.436,
     'L0_attn_bias_k': 64.0}
    for name, (base, spread) in spreads.items():
        noise = np.random.default_rng([zlib.crc32(name.encode()), seed]).standard_normal(out[name].shape)
        drawn = base * np.exp(spread * noise) if base else spread * noise
        out[name] = jnp.asarray(drawn.astype(out[name].dtype))
    for name, factor in factors.items():
        out[name] = (out[name] * factor).astype(out[name].dtype)
    return out
```

```python
import concourse.bass as bass
from concourse import mybir
from contextlib import ExitStack

B, T = 16, 120000
FRAME, STEP = 100, 160
NF = 1 + (T - FRAME) // STEP
BINS = FRAME // 2 + 1
NMEL, NMFCC = 40, 13
E, R, RM = 192, 96, 64
H, D = 12, 16
HG, G3 = 4, 3
TP, J = 125, 6
HC = 375
NX, I = 8, 96
NE1 = NX + 1
NFF = NE1 * I
CH = (NFF + 127) // 128
U = 2 * CH
ALPHA, LIMIT, EPS = 1.702, 7.0, 1e-5
XS = 1024.0
SLOTS = 6
QPARTS = ((0, 3, 0), (3, 2, 1), (5, 1, 2))
KPARTS = ((0, 3), (3, 2), (5, 1))
KROWS = SLOTS * D
MROWS = 3
TILES = HG * J
LEAD = TILES + 8
NPAIR = B * G3 * TILES
MT_AT = 18


class Chain:

    def __init__(self, eng, sem, per):
        self.eng, self.sem, self.k, self.per, self.m = eng, sem, 0, per, 0

    def begin(self, m):
        self.m, self.k = m, 0

    def link(self, ins):
        self.k += 1
        ins.then_inc(self.sem, 1)
        self.eng.wait_ge(self.sem, self.per * self.m + self.k)

    def end(self):
        assert self.per == self.k, (self.per, self.k)


def build(nc, x, melT, dct, w_proj, b_proj, vqT, uqh, vkT, uk, vvT, uv, bqh, bk, bv, muT, mv, gwT, gb,
          w1, b1, w3, b3, w2, b2, dft, ident, tri4, tri8, sel, out):
    fp32, bf16, fp16, i32 = mybir.dt.float32, mybir.dt.bfloat16, mybir.dt.float16, mybir.dt.int32
    ALU, ACT, AX = mybir.AluOpType, mybir.ActivationFunctionType, mybir.AxisListType
    ctx = ExitStack()
    with ctx:
        def sb(name, shape, dt):
            return ctx.enter_context(nc.sbuf_tensor(name, shape, dt))

        def sem(name):
            return ctx.enter_context(nc.semaphore(name))

        h0_dram = nc.dram_tensor("h0_scratch", (B, TP, J * E), fp32, kind="Internal").ap()
        qk_dram = nc.dram_tensor("qk_scratch", (2, 3, E, NF), bf16, kind="Internal").ap()

        idf = sb("idf", [128, 128], fp32)
        idb = sb("idb", [128, 128], bf16)
        big = sb("big", [128, 2 * HG * NF], fp32)
        probs = big[0:TP, :].rearrange("p (s h c) -> p s h c", s=2, h=HG)
        frames = big[0:TP, 0:4 * J * FRAME].rearrange("p (q j s) -> p q j s", q=4, j=J)
        o_ = 4 * J * FRAME
        frT = big[0:FRAME, o_:o_ + NF]
        power = big[0:FRAME, o_ + NF:o_ + 2 * NF]
        logm = big[0:64, o_ + 2 * NF:o_ + 3 * NF]
        h0t = sb("h0t", [TP, 2, J * E], fp32)
        hA = h0t[:, 0, :].rearrange("p (j e) -> p j e", j=J)
        hB = h0t[:, 1, :].rearrange("p (j e) -> p j e", j=J)
        hn1 = sb("hn1", [TP, J, 256], fp32)
        hP = hn1[:, :, 0:E]
        hn2 = sb("hn2", [TP, J, 256], fp32)
        qs = sb("qs", [128, G3, HG * NF], bf16)
        ks = sb("ks", [128, G3, HG * NF], bf16)
        parts = sb("parts", [128, 4, 3, NF], bf16)
        rest = sb("rest", [128, 2, NF], fp32)
        xA = sb("xA", [128, NF], fp32)
        xB = sb("xB", [128, NF], fp32)
        V = sb("V", [TP, G3, J, HG, 32], fp32)
        vtmp = sb("vtmp", [TP, G3, J, HG, 32], fp32)
        OT = sb("OT", [128, NF], fp32)
        x2Ah = sb("x2Ah", [128, NF], fp16)
        x2Al = sb("x2Al", [128, NF], fp16)
        x2B = sb("x2B", [128, NF], fp16)
        wAh = sb("wAh", [128, 2, 2 * NFF], fp16)
        wAl = sb("wAl", [128, 2, 2 * NFF], fp16)
        wBh = sb("wBh", [128, 2, 2 * NFF], fp16)
        wBl = sb("wBl", [128, 2, 2 * NFF], fp16)
        gwh = sb("gwh", [128, 2, NX], fp16)
        gwl = sb("gwl", [128, 2, NX], fp16)
        w2s = sb("w2s", [128, CH, E], fp32)
        b2s = sb("b2s", [NE1, E], fp32)
        wq = sb("wq", [128, 2, E], fp32)
        wk = sb("wk", [128, 2, E], fp32)
        wv = sb("wv", [128, 2, E], fp32)
        qb = sb("qb", [128, 4], fp32)
        bvb = sb("bvb", [TP, E], fp32)
        h1s = sb("h1s", [128, 2, 2, HC], fp32)
        hh = rest[:, 0, :].rearrange("p (n c) -> p n c", n=2)
        xg = sb("xg", [128, HC], fp32)
        xl = rest[:, 1, 0:HC]
        th = sb("th", [128, HC], fp32)
        ga = rest[:, 1, HC:NF]
        gt = sb("gt", [128, 2, HC], fp32)
        gg = sb("gg", [128, 3, HC], fp32)
        selb = sb("selb", [4 * NE1, CH * 128], bf16)
        cTb = sb("cTb", [4 * NE1, NF], bf16)
        cT = sb("cT", [NE1, NF], fp32)
        fb = sb("fb", [128, 6, 2 * CH], fp32)
        wmx = sb("wmx", [128, 12], fp32)
        wsc = sb("wsc", [128, 12], fp32)
        dfts = sb("dfts", [FRAME, FRAME], fp32)
        melS = sb("melS", [FRAME, NMEL], fp32)
        wc = sb("wc", [64, E], fp32)
        lneps = sb("lneps", [128, 1], fp32)
        neghalf = sb("neghalf", [TP, J], fp32)
        st = sb("st", [TP, J, 6], fp32)
        mvr = sb("mvr", [TP, J, 2], fp32)
        ve = sb("ve", [TP, J], fp32)
        rstd = sb("rstd", [TP, 2, J], fp32)
        negm = sb("negm", [TP, TILES], fp32)
        mres = sb("mres", [TP, TILES], fp32)
        mpart = sb("mpart", [TP, 3, TILES], bf16)
        mTs = sb("mTs", [3 * TILES, TP], bf16)
        rsum = sb("rsum", [TP, TILES], fp32)
        onrm = sb("onrm", [TP, TILES, D], fp32)
        lg = sb("lg", [TP, J, NX], fp32)
        sc = sb("sc", [TP, J, NX], fp32)
        sbia = sb("sbia", [TP, J, NX], fp32)
        rj = sb("rj", [TP, 4, J], fp32)
        r4 = sb("r4", [TP, 4, TILES], fp32)
        cmp1 = sb("cmp1", [TP, J, NX * NX], fp32)
        cmp2 = sb("cmp2", [TP, J, NX * NX], fp32)
        rank = sb("rank", [TP, J, NX], fp32)
        cw = sb("cw", [TP, J, 72], fp32)
        cres = sb("cres", [TP, J, NE1], fp32)
        cbf = sb("cbf", [TP, J, NE1], bf16)
        t4 = sb("t4", [TP, 16], fp32)
        t8 = sb("t8", [TP, 64], fp32)
        gbb = sb("gbb", [TP, NX], fp32)

        o_ = 0

        def tmp(rows, n):
            nonlocal o_
            o_ += n
            return big[0:rows, o_ - n:o_]
        wstage = tmp(128, 2 * NFF)
        vqT_s, vkT_s, vvT_s = tmp(R, E), tmp(R, E), tmp(R, E)
        uk_s, uv_s, uq2 = tmp(R, E), tmp(R, E), tmp(R, E)
        uqh_s = tmp(D, H * R)
        bqh_s = tmp(D, H)
        muT_s, mv_s = tmp(RM, D), tmp(RM, D)
        mm_s = tmp(D, D)
        dct_s, wp_s = tmp(NMFCC, NMEL), tmp(NMFCC, E)
        row = tmp(1, E)
        gstage = tmp(128, 2 * NX)
        sel_s = tmp(4 * NE1, CH * 128)
        assert o_ <= 2 * HG * NF

        ps = ctx.enter_context(nc.psum_tensor("ps", [128, 8, 512], fp32))

        def slot(s, rows=128, n=HC):
            return ps[0:rows, 2 * s:2 * s + 2, 0:n]

        const_loaded = sem("const_loaded")
        w_loaded, w_used = sem("w_loaded"), sem("w_used")
        setup_dve, setup_pe, setup_copied, setup_pool = sem("setup_dve"), sem("setup_pe"), sem("setup_copied"), sem("setup_pool")
        setup_amax = sem("setup_amax")
        fr_loaded = [sem(f"fr_loaded{i}") for i in range(4)]
        fr_turned, frT_ready, dft_done, power_ready = sem("fr_turned"), sem("frT_ready"), sem("dft_done"), sem("power_ready")
        mel_done, log_ready, h0_done, h0_copied = sem("mel_done"), sem("log_ready"), sem("h0_done"), sem("h0_copied")
        h0_stored = [sem(f"h0_stored{i}") for i in range(2)]
        hp_loaded, ha_loaded = sem("hp_loaded"), sem("ha_loaded")
        var1_ready, rstd1_ready, ln1_ready, x_turned = sem("var1_ready"), sem("rstd1_ready"), sem("ln1_ready"), sem("x_turned")
        xA_ready, xB_ready, proj_done, part1_ready = sem("xA_ready"), sem("xB_ready"), sem("proj_done"), sem("part1_ready")
        rest_ready, parts_ready, parts_stored, v_ready = sem("rest_ready"), sem("parts_ready"), sem("parts_stored"), sem("v_ready")
        v_copied = [sem(f"v_copied{g}") for g in range(G3)]
        stacks_loaded = [sem(f"stacks_loaded{g}") for g in range(G3)]
        maxrows_loaded = [sem(f"maxrows_loaded{g}") for g in range(G3)]
        a_done, max_done, b_done, exp_done, pv_done = sem("a_done"), sem("max_done"), sem("b_done"), sem("exp_done"), sem("pv_done")
        mparts_ready, max_turned, mT_ready = sem("mparts_ready"), sem("max_turned"), sem("mT_ready")
        o_copied, o_turned, norm_done = sem("o_copied"), sem("o_turned"), sem("norm_done")
        var2_ready, rstd2_ready, ln2_ready, hA_free = sem("var2_ready"), sem("rstd2_ready"), sem("ln2_ready"), sem("hA_free")
        x2_turned, x2hi_ready, x2lo_ready = sem("x2_turned"), sem("x2hi_ready"), sem("x2lo_ready")
        gate_done, logits_ready, gexp_ready, comb_ready = sem("gate_done"), sem("logits_ready"), sem("gexp_ready"), sem("comb_ready")
        comb_turned, combT_ready, comb_spread = sem("comb_turned"), sem("combT_ready"), sem("comb_spread")
        h1_done, h3_done, h1_copied, hh_ready = sem("h1_done"), sem("h3_done"), sem("h1_copied"), sem("hh_ready")
        xg_ready, tanh_ready, g_ready, w2_done = sem("xg_ready"), sem("tanh_ready"), sem("g_ready"), sem("w2_done")
        y_added, y_stored = sem("y_added"), sem("y_stored")
        ch_setup, ch_pre, ch_att, ch_norm, ch_ffn, ch_ln2 = (sem(n) for n in ("ch_setup", "ch_pre", "ch_att", "ch_norm", "ch_ffn", "ch_ln2"))

        def wait(eng, s, value):
            if not isinstance(value, int) or value > 0:
                eng.wait_ge(s, value)

        MUL, ADD, SUB, MAX, MIN = ALU.mult, ALU.add, ALU.subtract, ALU.max, ALU.min
        mel_T = melT
        const_loads = [
            (idf[:], ident), (dfts[:], dft), (melS[0:BINS, :], mel_T), (melS[BINS:FRAME, :], mel_T[1:BINS - 1, :]),
            (dct_s, dct), (wp_s, w_proj), (wc[NMEL:NMEL + 1, :], b_proj),
            (vqT_s, vqT), (vkT_s, vkT), (vvT_s, vvT), (uk_s, uk), (uv_s, uv), (uqh_s, uqh), (bqh_s, bqh), (muT_s, muT), (mv_s, mv),
            (qb[:, 2:3], bk[0:128, :]), (qb[0:E - 128, 3:4], bk[128:E, :]), (bvb[:], bv.broadcast_to([TP, E])),
            (fb[:, 0, :], b1), (fb[:, 1, :], b3), (b2s[:], b2),
            (w2s[:, 0:CH - 1, :], w2[0:128 * (CH - 1), :].rearrange("(c p) e -> p c e", p=128)),
            (w2s[0:NFF - 128 * (CH - 1), CH - 1, :], w2[128 * (CH - 1):NFF, :]),
            (t4[:], tri4.broadcast_to([TP, 16])), (t8[:], tri8.broadcast_to([TP, 64])), (gbb[:], gb.broadcast_to([TP, NX])),
            (sel_s, sel), (gstage[:, 0:NX], gwT[0:128, :]), (gstage[0:64, NX:2 * NX], gwT[128:E, :]), (gstage[64:128, NX:2 * NX], gwT[128:E, :]),
        ]
        wloads = [(0, w1, 0), (0, w1, 1), (1, w3, 0), (1, w3, 1)]
        wloads = wloads + wloads

        block = ctx.enter_context(nc.Block())

        @block.sync
        def _(sp):
            for dst, src in const_loads:
                sp.dma_start(dst, src).then_inc(const_loaded, 16)
            for n, (_, w, rem) in enumerate(wloads):
                wait(sp, w_used, n)
                if rem:
                    sp.dma_start(wstage[0:64, :], w[128:E, :]).then_inc(w_loaded, 16)
                    sp.dma_start(wstage[64:128, :], w[128:E, :]).then_inc(w_loaded, 16)
                else:
                    sp.dma_start(wstage[0:64, :], w[0:64, :]).then_inc(w_loaded, 16)
                    sp.dma_start(wstage[64:128, :], w[64:128, :]).then_inc(w_loaded, 16)
            sp.wait_ge(setup_dve, 1)
            sp.wait_ge(setup_pe, PE_SETUP)

            def load_frames(b, q):
                src = x[bass.ds(b, 1), :].rearrange("o (p j s) -> (o p) j s", p=TP, j=J)[:, :, 0:FRAME]
                sp.dma_start(frames[:, q], src).then_inc(fr_loaded[q], 16)

            def store_h0(b, q):
                sp.wait_ge(h0_copied, b + 1)
                dst = h0_dram[bass.ds(b, 1)].rearrange("o p e -> (o p) e")
                sp.dma_start(dst, h0t[:, q % 2, :]).then_inc(h0_stored[q % 2], 16)

            for q in range(4):
                load_frames(q, q)
            with sp.Fori(0, B // 4 - 1) as i:
                for q in range(4):
                    store_h0(4 * i + q, q)
                    load_frames(4 * i + q + 4, q)
            for q in range(4):
                store_h0(B - 4 + q, q)
            for q in range(2):
                sp.wait_ge(h0_stored[q], 16 * (B // 2))

            def store_parts(m):
                sp.wait_ge(parts_ready, 4 * (m + 1))
                for g in range(G3):
                    wait(sp, stacks_loaded[g], 192 * m)
                for t in range(4):
                    rows = 128 if t % 2 == 0 else E - 128
                    r0 = 128 * (t % 2)
                    dst = qk_dram[t // 2, :, r0:r0 + rows, :].rearrange("c f t -> f c t")
                    sp.dma_start(dst, parts[0:rows, t]).then_inc(parts_stored, 16)

            def load_stacks(m, g):
                free_at = None if isinstance(m, int) and m == 0 else sp.snap(72 * m + 24 * g - 48)
                if g == 0:
                    sp.wait_ge(parts_stored, 64 * (m + 1))
                if free_at is not None:
                    sp.wait_ge(b_done, free_at)
                h0 = g * HG * D
                for s0, n, part in QPARTS:
                    src = qk_dram[0, part, h0:h0 + HG * D, :].rearrange("(h d) t -> d h t", h=HG)
                    for s in range(s0, s0 + n):
                        sp.dma_start(qs[16 * s:16 * s + 16, g, :].rearrange("p (h t) -> p h t", h=HG), src).then_inc(stacks_loaded[g], 16)
                for s0, n in KPARTS:
                    for s in range(s0, s0 + n):
                        src = qk_dram[1, s - s0, h0:h0 + HG * D, :].rearrange("(h d) t -> d h t", h=HG)
                        sp.dma_start(ks[16 * s:16 * s + 16, g, :].rearrange("p (h t) -> p h t", h=HG), src).then_inc(stacks_loaded[g], 16)

            def load_maxrows(m, g):
                sp.wait_ge(mT_ready, 3 * m + g + 1)
                for c in range(3):
                    dst = qs[KROWS + c:KROWS + c + 1, g, :].rearrange("o (r t) -> o r t", r=TILES)
                    sp.dma_start(dst, mTs[TILES * c:TILES * c + TILES, :]).then_inc(maxrows_loaded[g], 16)

            def h0_row(m):
                return h0_dram[bass.ds(m, 1)].rearrange("o p (j e) -> (o p) j e", j=J)

            def load_hP(m):
                wait(sp, x_turned, 2 * m)
                sp.dma_start(hP, h0_row(m)).then_inc(hp_loaded, 16)

            def load_hA(m):
                wait(sp, hA_free, m)
                sp.dma_start(hA, h0_row(m)).then_inc(ha_loaded, 16)

            def copy_v(m, g):
                used_at = None if isinstance(m, int) and m == 0 else sp.snap(18 * m + 6 * g - 12)
                if g == 0:
                    sp.wait_ge(v_ready, m + 1)
                if used_at is not None:
                    sp.wait_ge(pv_done, used_at)
                sp.dma_start(V[:, g], vtmp[:, g]).then_inc(v_copied[g], 16)

            def store_y(m):
                for n in range(2):
                    sp.wait_ge(y_added, 2 * m + n + 1)
                    dst = out[bass.ds(m, 1)].rearrange("o (p j) e -> (o p) j e", j=J)[:, 3 * n:3 * n + 3, :]
                    sp.dma_start(dst, hB[:, 3 * n:3 * n + 3, :]).then_inc(y_stored, 16)

            def body(b, do_pre, do_ffn, more):
                if do_pre:
                    if more:
                        load_hP(b + 2)
                    store_parts(b + 1)
                if do_ffn:
                    load_hA(b)
                for g in range(G3):
                    if g < 2:
                        load_maxrows(b, g + 1)
                    elif do_pre:
                        load_maxrows(b + 1, 0)
                    if do_pre:
                        load_stacks(b + 1, g)
                        copy_v(b + 1, g)
                    if g == 0 and do_ffn:
                        store_y(b - 1)

            load_hP(0)
            load_hP(1)
            load_hA(0)
            store_parts(0)
            for g in range(G3):
                load_stacks(0, g)
                copy_v(0, g)
            load_maxrows(0, 0)
            body(0, True, False, True)
            with sp.Fori(1, B - 2) as b:
                body(b, True, True, True)
            body(B - 2, True, True, False)
            body(B - 1, False, True, False)
            store_y(B - 1)
            sp.wait_ge(y_stored, 32 * B)

        @block.gpsimd
        def _(pool):
            nc.gpsimd.memset(neghalf[:], -0.5).then_inc(setup_pool, 1)
            nc.gpsimd.memset(hn1[:, :, E:256], 0.0).then_inc(setup_pool, 1)
            nc.gpsimd.memset(vtmp[:], 0.0).then_inc(setup_pool, 1)
            nc.gpsimd.memset(cw[:], 0.0).then_inc(setup_pool, 1)
            pool.wait_ge(setup_pool, 4)
            nc.gpsimd.memset(vtmp[:, :, :, :, D:D + 1].rearrange("p g j h o -> p (g j h) o"), 1.0).then_inc(setup_pool, 1)
            nc.gpsimd.memset(cw[:, :, NX:NX + 1], 1.0).then_inc(setup_pool, 1)
            pool.wait_ge(setup_amax, 1)
            nc.gpsimd.partition_all_reduce(wsc[:, 0:3], wmx[:, 0:3], 128, bass.bass_isa.ReduceOp.max).then_inc(setup_pool, 1)

            def power_of(m, ready, done, which):
                pool.wait_ge(ready, m + 1)
                nc.gpsimd.tensor_tensor(rstd[:, which, :], ve[:], neghalf[:], op=ALU.pow).then_inc(done, 1)

            def body(b, do_pre, do_ffn):
                if do_pre:
                    power_of(b + 1, var1_ready, rstd1_ready, 0)
                if do_ffn:
                    power_of(b - 1, var2_ready, rstd2_ready, 1)

            power_of(0, var1_ready, rstd1_ready, 0)
            body(0, True, False)
            with pool.Fori(1, B - 1) as b:
                body(b, True, True)
            body(B - 1, False, True)
            power_of(B - 1, var2_ready, rstd2_ready, 1)

        @block.scalar
        def _(act):
            act.wait_ge(setup_dve, 1)
            with act.Fori(0, B) as b:
                act.wait_ge(dft_done, b + 1)
                act.wait_ge(mel_done, b)
                nc.scalar.activation(power.rearrange("p (n c) -> p n c", n=2), slot(1, FRAME), ACT.Square).then_inc(power_ready, 1)
                act.wait_ge(mel_done, b + 1)
                act.wait_ge(h0_done, b)
                nc.scalar.activation(logm[0:NMEL, :].rearrange("p (n c) -> p n c", n=2), slot(0, NMEL), ACT.Ln,
                                     bias=lneps[0:NMEL, :]).then_inc(log_ready, 1)

            def pre(m):
                act.wait_ge(x_turned, 2 * m + 1)
                wait(act, proj_done, 5 * m)
                nc.scalar.activation(xA[:].rearrange("p (n c) -> p n c", n=2), slot(0), ACT.Copy).then_inc(xA_ready, 1)
                wait(act, parts_stored, 64 * m)
                for t in range(4):
                    rows = 128 if t % 2 == 0 else E - 128
                    act.wait_ge(proj_done, 5 * m + t + 1)
                    nc.scalar.activation(parts[0:rows, t, 0, :].rearrange("p (n c) -> p n c", n=2), slot((2, 0, 1, 2)[t], rows),
                                         ACT.Identity, bias=qb[0:rows, t:t + 1]).then_inc(part1_ready, 1)

            def att(b, g):
                for k in range(TILES):
                    i, h = k // HG, k % HG
                    act.wait_ge(b_done, 72 * b + 24 * g + k + 1)
                    wait(act, pv_done, 18 * b + 6 * g + i - 1)
                    nc.scalar.activation(probs[:, i % 2, h, :].rearrange("p (n c) -> p n c", n=2),
                                         slot((2 * k + 1) % 3, TP), ACT.Exp).then_inc(exp_done, 1)
                act.wait_ge(pv_done, 18 * b + 6 * g + 6)
                wait(act, o_turned, 3 * b + g)
                nc.scalar.activation(OT[:].rearrange("p (n c) -> p n c", n=2), slot(3), ACT.Copy).then_inc(o_copied, 1)

            def ffn(m):
                act.wait_ge(x2_turned, 2 * m + 1)
                wait(act, h3_done, U * m)
                nc.scalar.activation(x2Ah[:].rearrange("p (n c) -> p n c", n=2), slot(0), ACT.Copy).then_inc(x2hi_ready, 1)
                act.wait_ge(x2_turned, 2 * m + 2)
                nc.scalar.activation(x2B[:].rearrange("p (n c) -> p n c", n=2), slot(1), ACT.Copy).then_inc(x2hi_ready, 1)
                act.wait_ge(logits_ready, m + 1)
                nc.scalar.activation(sc[:], lg[:], ACT.Exp).then_inc(gexp_ready, 1)

                def h1_copy(u):
                    c = u % CH
                    rows = min(128, NFF - 128 * c)
                    act.wait_ge(h1_done, U * m + u + 1)
                    if u >= 2:
                        act.wait_ge(hh_ready, U * m + u - 1)
                    for s in range(2):
                        ins = nc.scalar.activation(h1s[0:rows, u % 2, s, :], ps[0:rows, s, 0:HC], ACT.Identity,
                                                   bias=fb[0:rows, 2, s * CH + c:s * CH + c + 1], scale=wsc[0:rows, 8:9])
                    ins.then_inc(h1_copied, 1)

                for u in range(U):
                    c = u % CH
                    rows = min(128, NFF - 128 * c)
                    h1_copy(u)
                    act.wait_ge(xg_ready, U * m + u + 1)
                    nc.scalar.activation(th[0:rows, :], xg[0:rows, :], ACT.Tanh, scale=ALPHA / 2).then_inc(tanh_ready, 1)
                    if u == 0:
                        act.wait_ge(comb_turned, m + 1)
                        wait(act, comb_spread, U * m)
                        nc.scalar.activation(cTb[:].rearrange("p (n c) -> p n c", n=2), slot(3, 4 * NE1), ACT.Copy)
                        wait(act, w2_done, U * m)
                        nc.scalar.activation(cT[:].rearrange("p (n c) -> p n c", n=2), slot(3, NE1), ACT.Copy).then_inc(combT_ready, 1)

            def body(b, do_pre, do_ffn):
                if do_pre:
                    pre(b + 1)
                att(b, 0)
                if do_ffn:
                    ffn(b - 1)
                att(b, 1)
                att(b, 2)

            pre(0)
            body(0, True, False)
            with act.Fori(1, B - 1) as b:
                body(b, True, True)
            body(B - 1, False, True)
            ffn(B - 1)

        @block.vector
        def _(dve):
            V_ = nc.vector
            su = Chain(dve, ch_setup, 0)
            dve.wait_ge(const_loaded, 16 * len(const_loads))
            su.link(V_.memset(ks[KROWS:KROWS + 32, :, :].rearrange("p g c -> p (g c)"), 1.0))
            su.link(V_.memset(lneps[:], 1e-6))
            su.link(V_.tensor_copy(idb[:], idf[:]))
            for w in (wq, wk, wv):
                su.link(V_.memset(w[64:128, 1, :], 0.0))
            su.link(V_.tensor_copy(selb[:], sel_s))

            def setup_copy(n, dst, rows, cols, scale=1.0):
                dve.wait_ge(setup_pe, n)
                V_.tensor_scalar(dst, ps[0:rows, 7, 0:cols], scale, None, MUL).then_inc(setup_copied, 1)
            setup_copy(1, mm_s, D, D, float(D) ** -0.5)
            setup_copy(2, uq2, R, E)
            setup_copy(3, row, 1, E)
            setup_copy(4, qb[:, 0:1], 128, 1)
            setup_copy(5, qb[0:64, 1:2], 64, 1)
            n = 5
            for w in (wq, wk, wv):
                setup_copy(n + 1, w[:, 0, :], 128, E)
                setup_copy(n + 2, w[0:64, 1, :], 64, E)
                n += 2
            setup_copy(n + 1, wc[0:NMEL, :], NMEL, E)

            for k in range(4):
                dve.wait_ge(w_loaded, 32 * (k + 1))
                V_.tensor_reduce(wmx[:, 4 + k:5 + k], wstage, axis=AX.X, op=MAX, apply_absolute_value=True).then_inc(w_used, 1)
            dve.wait_ge(w_used, 4)
            su.link(V_.tensor_reduce(wmx[:, 0:1], wmx[:, 4:8], axis=AX.X, op=MAX))
            su.link(V_.tensor_reduce(wmx[:, 1:2], gstage, axis=AX.X, op=MAX, apply_absolute_value=True))
            V_.memset(wmx[:, 2:3], 1.0).then_inc(setup_amax, 1)
            dve.wait_ge(setup_pool, 7)
            su.link(V_.tensor_scalar(wsc[:, 0:3], wsc[:, 0:3], 1e-30, 1e30, MAX, MIN))
            su.link(V_.tensor_scalar(wsc[:, 3:6].bitcast(i32), wsc[:, 0:3].bitcast(i32), 0x7F800000, None, ALU.bitwise_and))
            su.link(V_.reciprocal(wsc[:, 9:12], wsc[:, 3:6]))
            su.link(V_.tensor_scalar(wsc[:, 9:12], wsc[:, 9:12], 8192.0, None, MUL))
            su.link(V_.tensor_scalar(wsc[:, 6:8], wsc[:, 3:5], 1.0 / (8192.0 * XS), None, MUL))
            su.link(V_.tensor_scalar(wsc[:, 8:9], wsc[:, 6:7], wsc[:, 6:7], None, MUL))
            su.link(V_.reciprocal(wsc[:, 2:3], wsc[:, 6:7]))
            su.link(V_.tensor_scalar(fb[:, 2, :], fb[:, 0, :], wsc[:, 6:7], None, MUL))
            su.link(V_.tensor_scalar(fb[:, 3, :], fb[:, 1, :], wsc[:, 2:3], None, MUL))
            for half in range(2):
                s_, h_, l_ = gstage[:, NX * half:NX * half + NX], gwh[:, half, :], gwl[:, half, :]
                su.link(V_.tensor_scalar(s_, s_, wsc[:, 10:11], None, MUL))
                su.link(V_.tensor_copy(h_, s_))
                su.link(V_.tensor_tensor(l_, s_, h_, op=SUB))
            for k in range(4, 8):
                which, _, rem = wloads[k]
                hi, lo = (wBh, wBl) if rem else (wAh, wAl)
                dve.wait_ge(w_loaded, 32 * (k + 1))
                su.link(V_.tensor_scalar(wstage, wstage, wsc[:, 9:10], None, MUL))
                su.link(V_.tensor_copy(hi[:, which, :], wstage))
                V_.tensor_tensor(lo[:, which, :], wstage, hi[:, which, :], op=SUB).then_inc(w_used, 1)
            dve.wait_ge(w_used, 8)
            dve.wait_ge(setup_copied, 12)
            dve.wait_ge(setup_pe, PE_SETUP)
            su.link(V_.memset(logm[32:64, :], 1.0))
            V_.memset(rsum[:], 1.0).then_inc(setup_dve, 1)

            with dve.Fori(0, B // 2) as i:
                for q in range(2):
                    b = 2 * i + q
                    dve.wait_ge(fr_turned, b + 1)
                    dve.wait_ge(dft_done, b)
                    V_.tensor_copy(frT.rearrange("p (n c) -> p n c", n=2), slot(0, FRAME)).then_inc(frT_ready, 1)
                    dve.wait_ge(h0_done, b + 1)
                    dve.wait_ge(h0_stored[q], 16 * i)
                    V_.tensor_copy(h0t[:, q, :].rearrange("p (n c) -> p n c", n=3), ps[0:TP, 4:7, 0:2 * E]).then_inc(h0_copied, 1)

            chp, cha, chn, chf, chl = (Chain(dve, s, n) for s, n in ((ch_pre, 6), (ch_att, 3), (ch_norm, 2), (ch_ffn, 2 + 3 * U + 26), (ch_ln2, 4)))

            def layernorm(ch, src, dst, var_ready, rstd_ready, which, m, scale):
                for j in range(J):
                    ins = V_.bn_stats(st[:, j, :], src[:, j, :])
                ch.link(ins)
                V_.memset(ve[:], 0.0)
                for j in range(J):
                    ins = V_.bn_aggr(mvr[:, j, :], st[:, j, :])
                ch.link(ins)
                V_.tensor_scalar(ve[:], mvr[:, :, 1], EPS, None, ADD).then_inc(var_ready, 1)
                dve.wait_ge(rstd_ready, m + 1)
                if scale != 1.0:
                    ch.link(V_.tensor_scalar(rstd[:, which, :], rstd[:, which, :], scale, None, MUL))
                for j in range(J):
                    ins = V_.tensor_scalar(dst[:, j, 0:E], src[:, j, :], mvr[:, j, 0:1], rstd[:, which, j:j + 1], SUB, MUL)
                return ins

            def pre(m):
                chp.begin(m)
                dve.wait_ge(hp_loaded, 16 * (m + 1))
                layernorm(chp, hP, hn1, var1_ready, rstd1_ready, 0, m, 1.0).then_inc(ln1_ready, 1)
                dve.wait_ge(x_turned, 2 * m + 2)
                V_.tensor_copy(xB[:].rearrange("p (n c) -> p n c", n=2), slot(1)).then_inc(xB_ready, 1)
                for t in range(4):
                    rows = 128 if t % 2 == 0 else E - 128
                    p_ = [parts[0:rows, t, c, :].rearrange("p (n c) -> p n c", n=2) for c in range(3)]
                    r_ = rest[0:rows, t % 2, :].rearrange("p (n c) -> p n c", n=2)
                    dve.wait_ge(part1_ready, 4 * m + t + 1)
                    V_.scalar_tensor_tensor(r_, slot((2, 0, 1, 2)[t], rows), qb[0:rows, t:t + 1], p_[0],
                                            op0=ADD, op1=SUB).then_inc(rest_ready, 1)
                    dve.wait_ge(rest_ready, 4 * m + t + 1)
                    chp.link(V_.tensor_copy(p_[1], r_))
                    V_.tensor_tensor(p_[2], r_, p_[1], op=SUB).then_inc(parts_ready, 1)
                dve.wait_ge(proj_done, 5 * m + 5)
                for g in range(G3):
                    wait(dve, v_copied[g], 16 * m)
                for j in range(J):
                    src = ps[0:TP, j // 2, E * (j % 2):E * (j % 2) + E].rearrange("p (g h d) -> p g h d", g=G3, h=HG)
                    ins = V_.tensor_tensor(vtmp[:, :, j, :, 0:D], src, bvb[:].rearrange("p (g h d) -> p g h d", g=G3, h=HG), op=ADD)
                ins.then_inc(v_ready, 1)
                chp.end()

            def amax(a, s, n):
                dve.wait_ge(a_done, a + 1)
                V_.tensor_reduce(negm[:, n:n + 1], slot(s, TP), axis=AX.XY, op=MAX, negate=True).then_inc(max_done, 1)

            def max_parts(G):
                cha.begin(G)
                dve.wait_ge(max_done, 24 * G + 24)
                wait(dve, max_turned, G)
                cha.link(V_.tensor_copy(mpart[:, 0, :], negm[:]))
                cha.link(V_.tensor_tensor(mres[:], negm[:], mpart[:, 0, :], op=SUB))
                cha.link(V_.tensor_copy(mpart[:, 1, :], mres[:]))
                V_.tensor_tensor(mpart[:, 2, :], mres[:], mpart[:, 1, :], op=SUB).then_inc(mparts_ready, 1)
                cha.end()

            def copy_mT(G, s, a, before):
                dve.wait_ge(max_turned, G + 1)
                if a is not None:
                    dve.wait_ge(a_done, a + 1)
                if before is not None:
                    dve.wait_ge(*before)
                V_.tensor_copy(mTs[:], ps[0:3 * TILES, 2 * s + 1, 384:384 + 63].bitcast(bf16)[:, 0:TP]).then_inc(mT_ready, 1)

            def norm(b, g):
                G = 3 * b + g
                chn.begin(G)
                dve.wait_ge(o_turned, G + 1)
                o4 = ps[0:TP, 6:8, 0:HC + 9].rearrange("p n (q c) -> p n q c", q=TILES // 2)
                chn.link(V_.reciprocal(rsum[:].rearrange("p (n q) -> p n q", n=2), o4[:, :, :, D]))
                for n in range(2):
                    ins = V_.tensor_tensor(onrm[:, 12 * n:12 * n + 12, :], o4[:, n, :, 0:D],
                                           rsum[:, 12 * n:12 * n + 12, None].broadcast_to([TP, 12, D]), op=MUL)
                ins.then_inc(norm_done, 1)
                dve.wait_ge(norm_done, G + 1)
                if g == 0:
                    dve.wait_ge(ha_loaded, 16 * (b + 1))
                v = hA[:, :, 64 * g:64 * g + 64]
                chn.link(V_.tensor_tensor(v, v, onrm[:].rearrange("p (j h) d -> p j (h d)", j=J), op=ADD))
                chn.end()

            def ln2(m):
                chl.begin(m)
                wait(dve, x2_turned, 2 * m)
                chl.link(layernorm(chl, hA, hn2, var2_ready, rstd2_ready, 1, m, XS))
                V_.tensor_copy(hn2[:, :, E:256], hn2[:, :, 128:E]).then_inc(ln2_ready, 1)
                wait(dve, y_stored, 32 * m)
                V_.tensor_copy(hB, hA).then_inc(hA_free, 1)
                dve.wait_ge(hA_free, m + 1)
                chl.end()

            def att(b, g, last_norm, do_ln2, a_tiles):
                for k in range(TILES):
                    if k == MT_AT and a_tiles > 15:
                        copy_mT(3 * b + g + 1, (2 * k) % 3, 72 * b + 24 * g + k + LEAD if k < a_tiles else None,
                                (maxrows_loaded[g], 48 * (b + 1)))
                    if k < a_tiles:
                        amax(72 * b + 24 * g + k + LEAD, (2 * k) % 3, (k + LEAD) % TILES)
                    if k == 15 and a_tiles > 15:
                        max_parts(3 * b + g + 1)
                    if k == 2 and last_norm is not None:
                        norm(*last_norm)
                        if do_ln2:
                            ln2(b - 1)

            def swiglu(m, u):
                c = u % CH
                rows = min(128, NFF - 128 * c)
                dve.wait_ge(h3_done, U * m + u + 1)
                dve.wait_ge(h1_copied, U * m + u + 1)
                for s in range(2):
                    ins = V_.scalar_tensor_tensor(hh[0:rows, s, :], ps[0:rows, 2 + s, 0:HC], fb[0:rows, 3, s * CH + c:s * CH + c + 1],
                                                  h1s[0:rows, u % 2, s, :], op0=ADD, op1=MUL)
                ins.then_inc(hh_ready, 1)
                dve.wait_ge(hh_ready, U * m + u + 1)
                V_.tensor_scalar(xg[0:rows, :], hh[0:rows, 0, :], LIMIT, None, MIN).then_inc(xg_ready, 1)
                chf.link(V_.tensor_scalar(xl[0:rows, :], hh[0:rows, 1, :], LIMIT, -LIMIT, MIN, MAX))

            def gate_product(m, u):
                c = u % CH
                rows = min(128, NFF - 128 * c)
                dve.wait_ge(xg_ready, U * m + u + 1)
                dve.wait_ge(tanh_ready, U * m + u + 1)
                chf.link(V_.scalar_tensor_tensor(ga[0:rows, :], th[0:rows, :], 1.0, xg[0:rows, :], op0=ADD, op1=MUL))
                chf.link(V_.scalar_tensor_tensor(gt[0:rows, u % 2, :], xl[0:rows, :], 1.0, ga[0:rows, :], op0=ADD, op1=MUL))

            def weigh(m, u):
                c = u % CH
                rows = min(128, NFF - 128 * c)
                dve.wait_ge(comb_spread, U * m + u + 1)
                if u >= 3:
                    dve.wait_ge(w2_done, U * m + u - 2)
                V_.tensor_tensor(gg[0:rows, u % 3, :], ps[0:rows, 4, 0:HC], gt[0:rows, u % 2, :], op=MUL).then_inc(g_ready, 1)

            def routing(m):
                L = chf.link
                dve.wait_ge(gexp_ready, m + 1)

                def over(t, n):
                    return t[:, :, None].broadcast_to([TP, J, n])
                L(V_.tensor_reduce(rj[:, 1, :], sc[:], axis=AX.X, op=ADD))
                L(V_.reciprocal(rj[:, 2, :], rj[:, 1, :]))
                L(V_.tensor_tensor(sc[:], sc[:], over(rj[:, 2, :], NX), op=MUL))
                L(V_.tensor_tensor(sbia[:], sc[:], gbb[:, None, :].broadcast_to([TP, J, NX]), op=ADD))
                L(V_.tensor_reduce(r4[:, 0, :], sbia[:].rearrange("p j (q t) -> p (j q) t", t=2), axis=AX.X, op=ADD))
                gs = r4[:, 0, :].rearrange("p (j q) -> p j q", j=J)

                def ranks(s, n, tri, dst):
                    c1 = cmp1[:, :, 0:n * n].rearrange("p j (a c) -> p j a c", a=n)
                    c2 = cmp2[:, :, 0:n * n].rearrange("p j (a c) -> p j a c", a=n)
                    other = s[:, :, None, :].broadcast_to([TP, J, n, n])
                    own = s[:, :, :, None].broadcast_to([TP, J, n, n])
                    L(V_.tensor_tensor(c1, other, own, op=ALU.is_gt))
                    L(V_.tensor_tensor(c2, other, own, op=ALU.is_equal))
                    L(V_.tensor_tensor(cmp2[:, :, 0:n * n], cmp2[:, :, 0:n * n], tri[:, None, :].broadcast_to([TP, J, n * n]), op=MUL))
                    L(V_.tensor_tensor(cmp1[:, :, 0:n * n], cmp1[:, :, 0:n * n], cmp2[:, :, 0:n * n], op=ADD))
                    L(V_.tensor_reduce(dst, c1, axis=AX.X, op=ADD))

                ranks(gs, 4, t4, r4[:, 1, :].rearrange("p (j q) -> p j q", j=J))
                L(V_.tensor_scalar(r4[:, 1, :], r4[:, 1, :], 2.0, None, ALU.is_lt))
                L(V_.tensor_scalar(r4[:, 2, :], r4[:, 1, :], 3.0e38, -3.0e38, MUL, ADD))
                s24 = sbia[:].rearrange("p j (q t) -> p (j q) t", t=2)
                L(V_.tensor_tensor(s24, s24, r4[:, 1, :, None].broadcast_to([TP, TILES, 2]), op=MUL))
                L(V_.tensor_tensor(s24, s24, r4[:, 2, :, None].broadcast_to([TP, TILES, 2]), op=ADD))
                ranks(sbia[:], NX, t8, rank[:])
                L(V_.tensor_scalar(rank[:], rank[:], 2.0, None, ALU.is_lt))
                wait(dve, comb_turned, m)
                L(V_.tensor_tensor(cw[:, :, 0:NX], sc[:], rank[:], op=MUL))
                c_ = cw[:, :, 0:NE1]
                L(V_.tensor_copy(cbf[:], c_))
                L(V_.tensor_copy(cw[:, :, NE1:2 * NE1], cbf[:]))
                L(V_.tensor_tensor(cres[:], c_, cbf[:], op=SUB))
                L(V_.tensor_copy(cbf[:], cres[:]))
                L(V_.tensor_copy(cw[:, :, 2 * NE1:3 * NE1], cbf[:]))
                V_.tensor_tensor(cw[:, :, 3 * NE1:4 * NE1], cres[:], cbf[:], op=SUB).then_inc(comb_ready, 1)

            def add_y(m, n):
                dve.wait_ge(w2_done, U * m + CH * (n + 1))
                v = hB[:, 3 * n:3 * n + 3, :]
                V_.tensor_tensor(v, ps[0:TP, 5:8, 0:E], v, op=ADD).then_inc(y_added, 1)

            def ffn(m):
                chf.begin(m)
                dve.wait_ge(x2hi_ready, 2 * m + 1)
                V_.tensor_tensor(x2Al[:].rearrange("p (n c) -> p n c", n=2), slot(0),
                                 x2Ah[:].rearrange("p (n c) -> p n c", n=2), op=SUB).then_inc(x2lo_ready, 1)
                dve.wait_ge(x2hi_ready, 2 * m + 2)
                v = x2B[64:128, :].rearrange("p (n c) -> p n c", n=2)
                V_.tensor_tensor(v, ps[64:128, 2:4, 0:HC], v, op=SUB).then_inc(x2lo_ready, 1)
                dve.wait_ge(gate_done, m + 1)
                chf.link(V_.tensor_scalar(lg[:], ps[0:TP, 4, 0:J * NX].rearrange("p (j e) -> p j e", j=J), wsc[0:TP, 7:8], None, MUL))
                chf.link(V_.tensor_reduce(rj[:, 0, :], lg[:], axis=AX.X, op=MAX))
                V_.tensor_tensor(lg[:], lg[:], rj[:, 0, :, None].broadcast_to([TP, J, NX]), op=SUB).then_inc(logits_ready, 1)
                for u in range(U):
                    swiglu(m, u)
                    if u == 0:
                        routing(m)
                    else:
                        weigh(m, u - 1)
                    gate_product(m, u)
                    if u == CH + 1:
                        add_y(m, 0)
                weigh(m, U - 1)
                add_y(m, 1)
                chf.end()

            def body(b, do_pre, do_ffn, a_tiles=(TILES, TILES, TILES)):
                if do_pre:
                    pre(b + 1)
                first = isinstance(b, int) and b == 0
                att(b, 0, None if first else (b - 1, 2), not first, a_tiles[0])
                if do_ffn:
                    ffn(b - 1)
                att(b, 1, (b, 0), False, a_tiles[1])
                att(b, 2, (b, 1), False, a_tiles[2])

            pre(0)
            for n in range(LEAD):
                if n == TILES + 2:
                    copy_mT(0, n % 3, n, None)
                amax(n, n % 3, n % TILES)
                if n == TILES - 1:
                    max_parts(0)
            body(0, True, False)
            with dve.Fori(1, B - 1) as b:
                body(b, True, True)
            body(B - 1, False, True, (TILES, NPAIR - LEAD - (NPAIR - 2 * TILES), 0))
            norm(B - 1, 2)
            ln2(B - 1)
            ffn(B - 1)

        @block.tensor
        def _(pe):
            def mm(o, l, r, start=True, stop=True):
                return nc.tensor.matmul(o, l, r, start=start, stop=stop)

            pe.wait_ge(const_loaded, 16 * len(const_loads))

            def b7(rows, c0, c1):
                return ps[0:rows, 7, c0:c1]
            mm(b7(D, 0, D), muT_s, mv_s).then_inc(setup_pe, 1)
            pe.wait_ge(setup_copied, 1)
            for h in range(H):
                ins = mm(b7(R, D * h, D * h + D), uqh_s[:, R * h:R * h + R], mm_s)
            ins.then_inc(setup_pe, 1)
            pe.wait_ge(setup_copied, 2)
            for h in range(H):
                ins = mm(b7(1, D * h, D * h + D), bqh_s[:, h:h + 1], mm_s)
            ins.then_inc(setup_pe, 1)
            pe.wait_ge(setup_copied, 3)
            mm(b7(128, 0, 1), row[:, 0:128], idf[0:1, 0:1]).then_inc(setup_pe, 1)
            pe.wait_ge(setup_copied, 4)
            mm(b7(64, 0, 1), row[:, 128:E], idf[0:1, 0:1]).then_inc(setup_pe, 1)
            n = 5
            for l, r in ((vqT_s, uq2), (vkT_s, uk_s), (vvT_s, uv_s)):
                pe.wait_ge(setup_copied, n)
                mm(b7(128, 0, E), l[:, 0:128], r).then_inc(setup_pe, 1)
                pe.wait_ge(setup_copied, n + 1)
                mm(b7(64, 0, E), l[:, 128:E], r).then_inc(setup_pe, 1)
                n += 2
            pe.wait_ge(setup_copied, n)
            mm(b7(NMEL, 0, E), dct_s, wp_s).then_inc(setup_pe, 1)
            pe.wait_ge(setup_copied, n + 1)
            pe.wait_ge(setup_dve, 1)

            def halves(s, rows, l, r):
                for q in range(2):
                    ins = mm(slot(s, rows)[:, q, :], l, r[:, HC * q:HC * q + HC])
                return ins

            with pe.Fori(0, B // 4) as i:
                for q in range(4):
                    b = 4 * i + q
                    pe.wait_ge(fr_loaded[q], 16 * (i + 1))
                    pe.wait_ge(log_ready, b)
                    for j in range(J):
                        ins = nc.tensor.transpose(ps[0:FRAME, j // 3, TP * (j % 3):TP * (j % 3) + TP], frames[:, q, j, :], idf[0:TP, 0:TP])
                    ins.then_inc(fr_turned, 1)
                    pe.wait_ge(frT_ready, b + 1)
                    halves(1, FRAME, dfts[:], frT).then_inc(dft_done, 1)
                    pe.wait_ge(power_ready, b + 1)
                    halves(0, NMEL, melS[:], power).then_inc(mel_done, 1)
                    pe.wait_ge(log_ready, b + 1)
                    pe.wait_ge(h0_copied, b)
                    for j in range(J):
                        ins = mm(ps[0:TP, 4 + j // 2, E * (j % 2):E * (j % 2) + E], logm[0:NMEL + 1, TP * j:TP * j + TP], wc[0:NMEL + 1, :])
                    ins.then_inc(h0_done, 1)
            pe.wait_ge(h0_copied, B)
            pe.wait_ge(log_ready, B)
            pe.wait_ge(power_ready, B)

            def turn(src, c0, s):
                for j in range(J):
                    ins = nc.tensor.transpose(ps[:, 2 * s + j // 3, TP * (j % 3):TP * (j % 3) + TP], src[:, j, c0:c0 + 128], idf[0:TP, 0:TP])
                return ins

            def pre(m):
                pe.wait_ge(ln1_ready, m + 1)
                turn(hn1, 0, 0).then_inc(x_turned, 1)
                turn(hn1, 128, 1).then_inc(x_turned, 1)
                pe.wait_ge(xA_ready, m + 1)
                pe.wait_ge(xB_ready, m + 1)
                for t, s in enumerate((2, 0, 1, 2)):
                    w = (wq, wk)[t // 2]
                    f0, rows = (0, 128) if t % 2 == 0 else (128, E - 128)
                    if t == 3:
                        pe.wait_ge(rest_ready, 4 * m + 1)
                    for q in range(2):
                        mm(slot(s, rows)[:, q, :], w[:, 0, f0:f0 + rows], xA[:, HC * q:HC * q + HC], True, False)
                        ins = mm(slot(s, rows)[:, q, :], w[:, 1, f0:f0 + rows], xB[:, HC * q:HC * q + HC], False, True)
                    ins.then_inc(proj_done, 1)
                pe.wait_ge(rest_ready, 4 * m + 3)
                for j in range(J):
                    o = ps[0:TP, j // 2, E * (j % 2):E * (j % 2) + E]
                    mm(o, xA[:, TP * j:TP * j + TP], wv[:, 0, :], True, False)
                    ins = mm(o, xB[:, TP * j:TP * j + TP], wv[:, 1, :], False, True)
                ins.then_inc(proj_done, 1)
                pe.wait_ge(v_ready, m + 1)
                pe.wait_ge(rest_ready, 4 * m + 4)

            def a_tile(g, n, s):
                h, j = n // J, n % J
                for q in range(2):
                    ins = mm(slot(s, TP)[:, q, :], qs[0:KROWS, g, NF * h + TP * j:NF * h + TP * j + TP],
                             ks[0:KROWS, g, NF * h + HC * q:NF * h + HC * q + HC])
                ins.then_inc(a_done, 1)

            def b_tile(g, k, s):
                i, h = k // HG, k % HG
                K = KROWS + MROWS
                for q in range(2):
                    ins = mm(slot(s, TP)[:, q, :], ks[0:K, g, NF * h + TP * i:NF * h + TP * i + TP],
                             qs[0:K, g, NF * h + HC * q:NF * h + HC * q + HC])
                ins.then_inc(b_done, 1)

            def turn_maxima(G, s):
                pe.wait_ge(mparts_ready, G + 1)
                nc.tensor.transpose(ps[0:3 * TILES, 2 * s + 1, 384:384 + 63].bitcast(bf16)[:, 0:TP],
                                    mpart[:].rearrange("p c r -> p (c r)"), idb[0:TP, 0:TP]).then_inc(max_turned, 1)

            def pv(b, g, i):
                pe.wait_ge(exp_done, 72 * b + 24 * g + 4 * i + 4)
                if i == 0:
                    wait(pe, norm_done, 3 * b + g)
                    pe.wait_ge(v_copied[g], 16 * (b + 1))
                for q in range(2):
                    for h in range(HG):
                        ins = mm(ps[32 * h:32 * h + 32, 6 + q, 0:HC], V[:, g, i, h, :], probs[:, i % 2, h, HC * q:HC * q + HC],
                                 i == 0, i == J - 1)
                ins.then_inc(pv_done, 1)

            def turn_outputs(G):
                pe.wait_ge(o_copied, G + 1)
                for j in range(J):
                    ins = nc.tensor.transpose(ps[0:TP, 6 + j // 3, 128 * (j % 3):128 * (j % 3) + 128], OT[:, TP * j:TP * j + TP], idf[:])
                ins.then_inc(o_turned, 1)

            def att(b, g, a_tiles, prev):
                t0 = 72 * b + 24 * g
                for k in range(TILES):
                    s = (2 * k) % 3
                    wait(pe, exp_done, t0 + k - 1)
                    if k == MT_AT and a_tiles > 15:
                        turn_maxima(3 * b + g + 1, s)
                    if k < a_tiles:
                        gn, n = (g + 1 + (k + 8) // TILES) % 3, (k + LEAD) % TILES
                        if n == 0:
                            pe.wait_ge(stacks_loaded[gn], 192 * (b + 1 + (1 if g + 2 > 2 else 0)))
                        a_tile(gn, n, s)
                    if k == 0:
                        pe.wait_ge(maxrows_loaded[g], 48 * (b + 1))
                    if k >= a_tiles + 1 or (a_tiles == 0):
                        wait(pe, exp_done, t0 + k - 2)
                    else:
                        pe.wait_ge(max_done, t0 + k + LEAD)
                    if k == MT_AT + 1 and a_tiles > 15:
                        pe.wait_ge(mT_ready, 3 * b + g + 2)
                    b_tile(g, k, (2 * k + 1) % 3)
                    if k == 1 and prev:
                        turn_outputs(3 * b + g - 1)
                    if k % HG == 0 and k > 0:
                        pv(b, g, k // HG - 1)
                pv(b, g, J - 1)

            def settle(b, g):
                pe.wait_ge(exp_done, 72 * b + 24 * g)
                pe.wait_ge(max_done, 72 * b + 24 * g + LEAD)
                pe.wait_ge(o_copied, 3 * b + g)

            def five(o, lo, hi, start=True, stop=True):
                xh, xlo, xb = lo
                wh, wl, wbh, wbl = hi
                mm(o, wh, xh, True, False)
                mm(o, wl, xh, False, False)
                mm(o, wh, xlo, False, False)
                mm(o, wbh, xb, False, False)
                return mm(o, wbl, xb, False, True)

            def ffn(m):
                pe.wait_ge(ln2_ready, m + 1)
                turn(hn2, 0, 0).then_inc(x2_turned, 1)
                turn(hn2, 128, 1).then_inc(x2_turned, 1)
                pe.wait_ge(x2hi_ready, 2 * m + 2)
                pe.wait_ge(x2lo_ready, 2 * m + 2)
                for j in range(J):
                    c = slice(TP * j, TP * j + TP)
                    o = ps[0:TP, 4, NX * j:NX * j + NX]
                    mm(o, x2Ah[:, c], gwh[:, 0, :], True, False)
                    mm(o, x2Ah[:, c], gwl[:, 0, :], False, False)
                    mm(o, x2Al[:, c], gwh[:, 0, :], False, False)
                    mm(o, x2B[:, c], gwh[:, 1, :], False, False)
                    ins = mm(o, x2B[:, c], gwl[:, 1, :], False, True)
                ins.then_inc(gate_done, 1)

                def first(u, which, s):
                    n, c = u // CH, u % CH
                    rows = min(128, NFF - 128 * c)
                    t = slice(HC * n, HC * n + HC)
                    for q in range(2):
                        f = slice(NFF * q + 128 * c, NFF * q + 128 * c + rows)
                        ins = five(slot(s, rows)[:, q, :], (x2Ah[:, t], x2Al[:, t], x2B[:, t]),
                                   (wAh[:, which, f], wAl[:, which, f], wBh[:, which, f], wBl[:, which, f]))
                    return ins

                def spread(u):
                    n, c = u // CH, u % CH
                    rows = min(128, NFF - 128 * c)
                    pe.wait_ge(combT_ready, m + 1)
                    wait(pe, g_ready, U * m + u)
                    mm(ps[0:rows, 4, 0:HC], selb[:, 128 * c:128 * c + rows], cTb[:, HC * n:HC * n + HC]).then_inc(comb_spread, 1)

                def second(u):
                    n, c = u // CH, u % CH
                    rows = min(128, NFF - 128 * c)
                    if c == 0:
                        if n == 1:
                            pe.wait_ge(y_added, 2 * m + 1)
                        for jj in range(3):
                            t = slice(HC * n + TP * jj, HC * n + TP * jj + TP)
                            mm(ps[0:TP, 5 + jj, 0:E], cT[:, t], b2s[:], True, False)
                    pe.wait_ge(g_ready, U * m + u + 1)
                    for jj in range(3):
                        ins = mm(ps[0:TP, 5 + jj, 0:E], gg[0:rows, u % 3, TP * jj:TP * jj + TP], w2s[0:rows, c, :], False, c == CH - 1)
                    ins.then_inc(w2_done, 1)

                for u in range(U):
                    wait(pe, h1_copied, U * m + u)
                    first(u, 0, 0).then_inc(h1_done, 1)
                    wait(pe, hh_ready, U * m + u)
                    first(u, 1, 1).then_inc(h3_done, 1)
                    if u == 0:
                        pe.wait_ge(comb_ready, m + 1)
                        for j in range(J):
                            ins = nc.tensor.transpose(ps[0:72, 6 + j // 3, TP * (j % 3):TP * (j % 3) + TP], cw[:, j, :], idf[0:TP, 0:TP])
                        ins.then_inc(comb_turned, 1)
                    else:
                        spread(u - 1)
                        if u > 1:
                            second(u - 2)
                spread(U - 1)
                second(U - 2)
                second(U - 1)
                pe.wait_ge(y_added, 2 * m + 2)

            def body(b, do_pre, do_ffn, a_tiles=(TILES, TILES, TILES)):
                first_row = isinstance(b, int) and b == 0
                if do_pre:
                    if not first_row:
                        settle(b, 0)
                    else:
                        pe.wait_ge(max_done, LEAD)
                    pre(b + 1)
                att(b, 0, a_tiles[0], not first_row)
                if do_ffn:
                    settle(b, 1)
                    ffn(b - 1)
                att(b, 1, a_tiles[1], True)
                att(b, 2, a_tiles[2], True)

            pre(0)
            for n in range(LEAD):
                if n % TILES == 0:
                    pe.wait_ge(stacks_loaded[n // TILES], 192)
                wait(pe, max_done, n - 2)
                if n == TILES + 2:
                    turn_maxima(0, n % 3)
                a_tile(n // TILES, n % TILES, n % 3)
            body(0, True, False)
            with pe.Fori(1, B - 1) as b:
                body(b, True, True)
            body(B - 1, False, True, (TILES, NPAIR - LEAD - (NPAIR - 2 * TILES), 0))
            pe.wait_ge(exp_done, NPAIR)
            turn_outputs(3 * B - 1)
            pe.wait_ge(norm_done, 3 * B)
            ffn(B - 1)


PE_SETUP = 12


def kernel(**inputs):
    import numpy as np
    import concourse.bacc as bacc
    from concourse.bass_utils import run_bass_kernel_spmd

    def a(name):
        return np.asarray(inputs[name])

    def both(per_expert, shared):
        cols = []
        for s in range(2):
            p = per_expert[:, :, s::2]
            cols += [p.transpose(1, 0, 2).reshape(p.shape[1], NX * I), shared[:, s::2]]
        return np.concatenate(cols, axis=1)

    def by_chunk(bias):
        z = np.zeros((2, CH * 128), bias.dtype)
        z[:, 0:NFF] = bias.reshape(2, NFF)
        return z.reshape(2 * CH, 128).T

    s = np.arange(FRAME)
    window = 0.54 - 0.46 * np.cos(2.0 * np.pi * s / (FRAME - 1))
    k = np.arange(BINS)
    angle = 2.0 * np.pi * np.outer(s, k) / FRAME
    dft = (window[:, None] * np.concatenate([np.cos(angle), np.sin(angle[:, 1:BINS - 1])], axis=1)).astype(np.float32)
    sel = np.zeros((4 * NE1, CH * 128), np.float32)
    for c in range(3):
        for f in range(NFF):
            sel[NE1 * (c + 1) + f // I, f] = 0.5

    p = "L0_attn_"
    f = "L0_ffn_"
    arrays = dict(
        x=a("x"), melT=a("L0_tok_mel_filters").T, dct=a("L0_tok_dct"), w_proj=a("L0_tok_w_proj"), b_proj=a("L0_tok_b_proj")[None],
        vqT=a(p + "V_Q").T, uqh=a(p + "U_Q").reshape(R, H, D).transpose(2, 1, 0).reshape(D, H * R),
        vkT=a(p + "V_K").T, uk=a(p + "U_K"), vvT=a(p + "V_V").T, uv=a(p + "U_V"),
        bqh=a(p + "bias_q").reshape(H, D).T, bk=a(p + "bias_k")[:, None], bv=a(p + "bias_v")[None],
        muT=a(p + "M_U").T, mv=a(p + "M_V"), gwT=a(f + "gate_w").T, gb=a(f + "gate_b")[None],
        w1=both(a(f + "W1"), a(f + "Ws1")), b1=by_chunk(both(a(f + "B1")[:, None, :], a(f + "Bs1")[None])),
        w3=both(a(f + "W3"), a(f + "Ws3")), b3=by_chunk(both(a(f + "B3")[:, None, :], a(f + "Bs3")[None])),
        w2=np.concatenate([a(f + "W2").reshape(NX * I, E), a(f + "Ws2")]), b2=np.concatenate([a(f + "B2"), a(f + "Bs2")[None]]),
        dft=dft, ident=np.eye(128, dtype=np.float32),
        tri4=np.tri(4, 4, -1, dtype=np.float32).reshape(1, 16), tri8=np.tri(8, 8, -1, dtype=np.float32).reshape(1, 64), sel=sel,
    )
    nc = bacc.Bacc("TRN2", target_bir_lowering=False, num_devices=1)
    fed, aps = {}, {}
    for name, v in arrays.items():
        v = np.ascontiguousarray(v)
        fed["in_" + name] = v
        aps[name] = nc.dram_tensor("in_" + name, v.shape, mybir.dt.from_np(v.dtype), kind="ExternalInput").ap()
    aps["out"] = nc.dram_tensor("out", (B, NF, E), mybir.dt.float32, kind="ExternalOutput").ap()
    build(nc, **aps)
    return run_bass_kernel_spmd(nc, [fed], core_ids=[0]).results[0]["out"]
```

```python
import concourse.bass as bass
from concourse import mybir
from contextlib import ExitStack
import itertools

B, T = 16, 120000
FRAME, STEP = 100, 160
NF = 1 + (T - FRAME) // STEP
BINS = FRAME // 2 + 1
NMEL, NMFCC = 40, 13
E, R, RM = 192, 96, 64
H, D = 12, 16
HG, G3 = 4, 3
TP, J = 125, 6
HC = 375
NX, I = 8, 96
NE1 = NX + 1
NFF = NE1 * I
CH = (NFF + 127) // 128
U = 2 * CH
ALPHA, LIMIT, EPS = 1.702, 7.0, 1e-5
XS = 1024.0
SLOTS = 6
QPARTS = ((0, 3, 0), (3, 2, 1), (5, 1, 2))
KPARTS = ((0, 3), (3, 2), (5, 1))
KROWS = SLOTS * D
MROWS = 3
TILES = HG * J
LEAD = TILES + 8
NPAIR = B * G3 * TILES
PV_COLS = ((0, 188), (188, 375), (375, 563), (563, 750))
PV_FROM = HG + 1
PV_LAST = range(len(PV_COLS) * (J - 1), len(PV_COLS) * J)
TURN_O = 3
MT_AT = 18
NPRE, NPREP = 9, 3
PRE_AFTER = {2: (0, 1), 6: (2,), 8: (3,), 10: (4,), 12: (5,), 14: (6,), 16: (7,), 19: (8,)}
PRE_RESTS = {k + 1: tiles[0] - 2 for k, tiles in PRE_AFTER.items() if 2 <= tiles[0] < 6}
PREP_AFTER = {14: (0, 1), 19: (2,)}


def schedule(prep=False, pre=None, a_tiles=TILES):
    tiles = []
    for k in range(TILES):
        tiles.append(("A", k) if k < a_tiles else ("M", k) if k == MT_AT and a_tiles > 15 else None)
        tiles.append(("B", k))
        if prep:
            tiles += [("F", i) for i in PREP_AFTER.get(k, ())]
        if pre is not None:
            tiles += [("P", i, pre) for i in PRE_AFTER.get(k, ())]
    assert len(tiles) % 3 == 0
    return tiles


def first_schedule():
    tiles = [("P", i, 0) for i in range(NPRE)]
    tiles += [("P", i, 1) for i in range(NPRE)]
    tiles += [("A", n - LEAD) for n in range(LEAD)] + [None]
    assert len(tiles) % 3 == 0
    return tiles


class Chain:

    def __init__(self, eng, sem, per):
        self.eng, self.sem, self.k, self.per, self.m = eng, sem, 0, per, 0

    def begin(self, m):
        self.m, self.k = m, 0

    def link(self, ins):
        self.k += 1
        ins.then_inc(self.sem, 1)
        self.eng.wait_ge(self.sem, self.per * self.m + self.k)

    def end(self):
        assert self.per == self.k, (self.per, self.k)


def build(nc, x, melT, dct, w_proj, b_proj, vqT, uqh, vkT, uk, vvT, uv, bqh, bk, bv, muT, mv, gwT, gb,
          w1, b1, w3, b3, w2, b2, dft, ident, tri4, tri8, sel, out):
    fp32, bf16, fp16, i32 = mybir.dt.float32, mybir.dt.bfloat16, mybir.dt.float16, mybir.dt.int32
    ALU, ACT, AX = mybir.AluOpType, mybir.ActivationFunctionType, mybir.AxisListType
    ctx = ExitStack()
    with ctx:
        def sb(name, shape, dt):
            return ctx.enter_context(nc.sbuf_tensor(name, shape, dt))

        def sem(name):
            return ctx.enter_context(nc.semaphore(name))

        h0_dram = nc.dram_tensor("h0_scratch", (B, TP, J * E), fp32, kind="Internal").ap()
        qk_dram = nc.dram_tensor("qk_scratch", (B, 2, 3, E, NF), bf16, kind="Internal").ap()
        v_dram = nc.dram_tensor("v_scratch", (B, TP, J * H * 32), fp32, kind="Internal").ap()

        idf = sb("idf", [128, 128], fp32)
        idb = sb("idb", [128, 128], bf16)
        big = sb("big", [128, 2 * HG * NF], fp32)
        probs = big[0:TP, :].rearrange("p (s h c) -> p s h c", s=2, h=HG)
        frames = big[0:TP, 0:4 * J * FRAME].rearrange("p (q j s) -> p q j s", q=4, j=J)
        o_ = 4 * J * FRAME
        frT = big[0:FRAME, o_:o_ + NF]
        power = big[0:FRAME, o_ + NF:o_ + 2 * NF]
        logm = big[0:64, o_ + 2 * NF:o_ + 3 * NF]
        h0t = sb("h0t", [TP, 2, J * E], fp32)
        hA = h0t[:, 0, :].rearrange("p (j e) -> p j e", j=J)
        hB = h0t[:, 1, :].rearrange("p (j e) -> p j e", j=J)
        hn1 = sb("hn1", [TP, J, 256], fp32)
        hP = hn1[:, :, 0:E]
        hn2 = sb("hn2", [TP, J, 256], fp32)
        qs = sb("qs", [128, G3, HG * NF], bf16)
        ks = sb("ks", [128, G3, HG * NF], bf16)
        parts = sb("parts", [128, 4, 3, NF], bf16)
        rest = sb("rest", [128, 2, NF], fp32)
        xA = sb("xA", [128, NF], fp32)
        xB = sb("xB", [128, NF], fp32)
        V = sb("V", [TP, G3, J, HG, 32], fp32)
        vtmp = sb("vtmp", [TP, J, H, 32], fp32)
        OT = sb("OT", [128, NF], fp32)
        x2Ah = sb("x2Ah", [128, NF], fp16)
        x2Al = sb("x2Al", [128, NF], fp16)
        x2B = sb("x2B", [128, NF], fp16)
        wAh = sb("wAh", [128, 2, 2 * NFF], fp16)
        wAl = sb("wAl", [128, 2, 2 * NFF], fp16)
        wBh = sb("wBh", [128, 2, 2 * NFF], fp16)
        wBl = sb("wBl", [128, 2, 2 * NFF], fp16)
        gwh = sb("gwh", [128, 2, NX], fp16)
        gwl = sb("gwl", [128, 2, NX], fp16)
        w2s = sb("w2s", [128, CH, E], fp32)
        b2s = sb("b2s", [NE1, E], fp32)
        wq = sb("wq", [128, 2, E], fp32)
        wk = sb("wk", [128, 2, E], fp32)
        wv = sb("wv", [128, 2, E], fp32)
        h1s = sb("h1s", [128, 2, 2, HC], fp32)
        hh = rest[:, 0, :].rearrange("p (n c) -> p n c", n=2)
        xg = sb("xg", [128, HC], fp32)
        xl = rest[:, 1, 0:HC]
        th = sb("th", [128, HC], fp32)
        ga = rest[:, 1, HC:NF]
        gt = sb("gt", [128, 2, HC], fp32)
        gg = sb("gg", [128, 3, HC], fp32)
        selb = sb("selb", [4 * NE1, CH * 128], bf16)
        cTb = sb("cTb", [4 * NE1, NF], bf16)
        cT = sb("cT", [NE1, NF], fp32)
        fb = sb("fb", [128, 6, 2 * CH], fp32)
        wmx = sb("wmx", [128, 12], fp32)
        wsc = sb("wsc", [128, 12], fp32)
        dfts = sb("dfts", [FRAME, FRAME], fp32)
        melS = sb("melS", [FRAME, NMEL], fp32)
        wc = sb("wc", [64, E], fp32)
        lneps = sb("lneps", [128, 1], fp32)
        neghalf = sb("neghalf", [TP, J], fp32)
        idle = sb("idle", [1, 64], fp32)
        negone = sb("negone", [TP, J], fp32)
        st = sb("st", [TP, J, 6], fp32)
        mvr = sb("mvr", [TP, J, 2], fp32)
        ve = sb("ve", [TP, J], fp32)
        nmean = sb("nmean", [TP, J], fp32)
        nmr = sb("nmr", [TP, J], fp32)
        rstd = sb("rstd", [TP, 2, J], fp32)
        negm = sb("negm", [TP, TILES], fp32)
        mres = sb("mres", [TP, TILES], fp32)
        mpart = sb("mpart", [TP, 3, TILES], bf16)
        mTs = sb("mTs", [3 * TILES, TP], bf16)
        rsum = sb("rsum", [TP, TILES], fp32)
        onrm = sb("onrm", [TP, TILES, D], fp32)
        lg = sb("lg", [TP, J, NX], fp32)
        sc = sb("sc", [TP, J, NX], fp32)
        sbia = sb("sbia", [TP, J, NX], fp32)
        rj = sb("rj", [TP, 4, J], fp32)
        r4 = sb("r4", [TP, 4, TILES], fp32)
        cmp1 = sb("cmp1", [TP, J, NX * NX], fp32)
        cmp2 = sb("cmp2", [TP, J, NX * NX], fp32)
        rank = sb("rank", [TP, J, NX], fp32)
        cw = sb("cw", [TP, J, 72], fp32)
        cres = sb("cres", [TP, J, NE1], fp32)
        cbf = sb("cbf", [TP, J, NE1], bf16)
        t4 = sb("t4", [TP, 16], fp32)
        t8 = sb("t8", [TP, 64], fp32)
        gbb = sb("gbb", [TP, NX], fp32)

        o_ = 0
        scratch = parts[:].rearrange("p t c n -> p (t c n)").bitcast(fp32)
        wst = [qs[:].rearrange("p g c -> p (g c)").bitcast(fp32)[:, 2 * NFF * i:2 * NFF * i + 2 * NFF] for i in range(2)]

        def tmp(rows, n):
            nonlocal o_
            o_ += n
            return scratch[0:rows, o_ - n:o_]
        vqT_s, vkT_s, vvT_s = tmp(R, E), tmp(R, E), tmp(R, E)
        uk_s, uv_s, uq2 = tmp(R, E), tmp(R, E), tmp(R, E)
        uqh_s = tmp(D, H * R)
        bqh_s = tmp(D, H)
        muT_s, mv_s = tmp(RM, D), tmp(RM, D)
        mm_s = tmp(D, D)
        dct_s, wp_s = tmp(NMFCC, NMEL), tmp(NMFCC, E)
        gstage = tmp(128, 2 * NX)
        sel_s = tmp(4 * NE1, CH * 128)
        assert o_ <= 4 * 3 * NF // 2

        ps = ctx.enter_context(nc.psum_tensor("ps", [128, 8, 512], fp32))

        def slot(s, rows=128, n=HC):
            return ps[0:rows, 2 * s:2 * s + 2, 0:n]

        tok_loaded, const_loaded, late_loaded = sem("tok_loaded"), sem("const_loaded"), sem("late_loaded")
        w_loaded, w_seen, w_split = [sem(f"w_loaded{i}") for i in range(2)], sem("w_seen"), sem("w_split")
        setup_dve, setup_pe, setup_copied, setup_pool = sem("setup_dve"), sem("setup_pe"), sem("setup_copied"), sem("setup_pool")
        setup_amax, scales_ready, ch_pool = sem("setup_amax"), sem("scales_ready"), sem("ch_pool")
        fr_loaded = [sem(f"fr_loaded{i}") for i in range(4)]
        fr_turned, frT_ready, dft_done, power_ready = sem("fr_turned"), sem("frT_ready"), sem("dft_done"), sem("power_ready")
        mel_done, log_ready, h0_done, h0_copied = sem("mel_done"), sem("log_ready"), sem("h0_done"), sem("h0_copied")
        h0_stored = [sem(f"h0_stored{i}") for i in range(2)]
        hp_loaded, ha_loaded = sem("hp_loaded"), sem("ha_loaded")
        var1_ready, ln1_ready, x_turned = sem("var1_ready"), sem("ln1_ready"), sem("x_turned")
        xA_ready, xB_ready, proj_done, part1_ready = sem("xA_ready"), sem("xB_ready"), sem("proj_done"), sem("part1_ready")
        raw_ready, rest_ready, part2_ready, parts_ready = sem("raw_ready"), sem("rest_ready"), sem("part2_ready"), sem("parts_ready")
        parts_stored, v_ready, v_stored = sem("parts_stored"), sem("v_ready"), sem("v_stored")
        v_loaded = [sem(f"v_loaded{g}") for g in range(G3)]
        stacks_loaded = [sem(f"stacks_loaded{g}") for g in range(G3)]
        maxrows_loaded = [sem(f"maxrows_loaded{g}") for g in range(G3)]
        a_done, max_done, b_done, exp_done, pv_done = sem("a_done"), sem("max_done"), sem("b_done"), sem("exp_done"), sem("pv_done")
        mparts_ready, max_turned, mT_ready = sem("mparts_ready"), sem("max_turned"), sem("mT_ready")
        o_copied, o_turned, norm_done = sem("o_copied"), sem("o_turned"), sem("norm_done")
        var2_ready, rstd2_ready, ln2_ready, hA_free = sem("var2_ready"), sem("rstd2_ready"), sem("ln2_ready"), sem("hA_free")
        x2_turned, x2raw_ready, x2hi_ready, x2lo_ready = sem("x2_turned"), sem("x2raw_ready"), sem("x2hi_ready"), sem("x2lo_ready")
        gate_done, gate_read, logits_ready, gexp_ready, comb_ready = sem("gate_done"), sem("gate_read"), sem("logits_ready"), sem("gexp_ready"), sem("comb_ready")
        comb_turned, combT_ready, comb_spread = sem("comb_turned"), sem("combT_ready"), sem("comb_spread")
        h1_done, h3_done, h1_copied, hh_ready = sem("h1_done"), sem("h3_done"), sem("h1_copied"), sem("hh_ready")
        xg_ready, tanh_ready, g_ready, w2_done = sem("xg_ready"), sem("tanh_ready"), sem("g_ready"), sem("w2_done")
        y_added, y_stored = sem("y_added"), sem("y_stored")
        h_added, pow2_done, ch_route, ch_ln1, ch_dup = (sem(n) for n in ("h_added", "pow2_done", "ch_route", "ch_ln1", "ch_dup"))
        ch_setup, ch_pre, ch_att, ch_norm, ch_ffn, ch_ln2 = (sem(n) for n in ("ch_setup", "ch_pre", "ch_att", "ch_norm", "ch_ffn", "ch_ln2"))

        def wait(eng, s, value):
            if not isinstance(value, int) or value > 0:
                eng.wait_ge(s, value)

        MUL, ADD, SUB, MAX, MIN = ALU.mult, ALU.add, ALU.subtract, ALU.max, ALU.min
        tok_loads = [
            (idf[:], ident), (dfts[:], dft), (melS[0:BINS, :], melT), (melS[BINS:FRAME, :], melT[1:BINS - 1, :]),
            (dct_s, dct), (wp_s, w_proj), (wc[NMEL:NMEL + 1, :], b_proj),
        ]
        const_loads = [
            (muT_s, muT), (mv_s, mv), (uqh_s, uqh), (bqh_s, bqh), (vqT_s, vqT), (vkT_s, vkT), (uk_s, uk), (vvT_s, vvT), (uv_s, uv),
            (wk[64:65, 1, :], bk), (wv[64:65, 1, :], bv),
        ]
        late_loads = [
            (gstage[:, 0:NX], gwT[0:128, :]), (gstage[0:64, NX:2 * NX], gwT[128:E, :]), (gstage[64:128, NX:2 * NX], gwT[128:E, :]),
            (sel_s, sel), (fb[:, 0, :], b1), (fb[:, 1, :], b3), (b2s[:], b2),
            (w2s[:, 0:CH - 1, :], w2[0:128 * (CH - 1), :].rearrange("(c p) e -> p c e", p=128)),
            (w2s[0:NFF - 128 * (CH - 1), CH - 1, :], w2[128 * (CH - 1):NFF, :]),
            (t4[:], tri4.broadcast_to([TP, 16])), (t8[:], tri8.broadcast_to([TP, 64])), (gbb[:], gb.broadcast_to([TP, NX])),
        ]
        wloads = [(0, w1, 0), (0, w1, 1), (1, w3, 0), (1, w3, 1)] * 2

        def tile_read(tile, b, g):
            kind, k = tile[0], tile[1]
            if kind == "A":
                return max_done, 72 * b + 24 * g + k + LEAD + 1
            if kind == "B":
                return exp_done, 72 * b + 24 * g + k + 1
            if kind == "M":
                return mT_ready, 3 * b + g + 2
            if kind == "F":
                return (x2raw_ready, 2 * (b - 1) + k + 1) if k < 2 else (gate_read, b)
            m = b + tile[2]
            if k < 2:
                return (xA_ready, xB_ready)[k], m + 1
            return (raw_ready, 4 * m + k - 1) if k < 6 else (v_ready, 3 * m + k - 5)

        PLAIN, FIRST = schedule(), first_schedule()
        SECTIONS = (schedule(prep=True), PLAIN, schedule(pre=2))
        LAST_A = 2 * TILES - LEAD

        def in_slot(tiles):
            return [(tile, p % 3) for p, tile in enumerate(tiles) if tile is not None]

        block = ctx.enter_context(nc.Block())

        @block.sync
        def _(sp):
            def load_frames(b, q):
                src = x[bass.ds(b, 1), :].rearrange("o (p j s) -> (o p) j s", p=TP, j=J)[:, :, 0:FRAME]
                sp.dma_start(frames[:, q], src).then_inc(fr_loaded[q], 16)

            def store_h0(b, q):
                sp.wait_ge(h0_copied, b + 1)
                dst = h0_dram[bass.ds(b, 1)].rearrange("o p e -> (o p) e")
                sp.dma_start(dst, h0t[:, q % 2, :]).then_inc(h0_stored[q % 2], 16)

            load_frames(0, 0)
            for dst, src in tok_loads[:3]:
                sp.dma_start(dst, src).then_inc(tok_loaded, 16)
            for q in range(1, 4):
                load_frames(q, q)
            for dst, src in late_loads:
                sp.dma_start(dst, src).then_inc(late_loaded, 16)
            for q in range(4):
                store_h0(q, q)
                load_frames(q + 4, q)
            sp.wait_ge(h0_stored[0], 16)
            sp.dma_start(hP, h0_dram[0].rearrange("p (j e) -> p j e", j=J)).then_inc(hp_loaded, 16)
            with sp.Fori(1, B // 4 - 1) as i:
                for q in range(4):
                    store_h0(4 * i + q, q)
                    load_frames(4 * i + q + 4, q)
            for q in range(4):
                store_h0(B - 4 + q, q)
            for q in range(2):
                sp.wait_ge(h0_stored[q], 16 * (B // 2))

            def h0_row(m):
                return h0_dram[bass.ds(m, 1)].rearrange("o p (j e) -> (o p) j e", j=J)

            def load_hP(m):
                wait(sp, x_turned, 2 * m)
                sp.dma_start(hP, h0_row(m)).then_inc(hp_loaded, 16)

            def load_hA(m):
                wait(sp, hA_free, m)
                wait(sp, ln2_ready, m)
                sp.dma_start(hA, h0_row(m)).then_inc(ha_loaded, 16)

            def store_parts(m):
                sp.wait_ge(parts_ready, 4 * (m + 1))
                for t in range(4):
                    rows = 128 if t % 2 == 0 else E - 128
                    r0 = 128 * (t % 2)
                    dst = qk_dram[bass.ds(m, 1), t // 2, :, r0:r0 + rows, :].rearrange("o c f t -> (o f) c t")
                    sp.dma_start(dst, parts[0:rows, t]).then_inc(parts_stored, 16)

            def store_v(m):
                sp.wait_ge(v_ready, 3 * (m + 1))
                dst = v_dram[bass.ds(m, 1)].rearrange("o p c -> (o p) c")
                sp.dma_start(dst, vtmp[:].rearrange("p j h c -> p (j h c)")).then_inc(v_stored, 16)

            def load_stacks(m, g):
                free_at = None if isinstance(m, int) and m == 0 else sp.snap(72 * m + 24 * g - 48)
                used_at = None if isinstance(m, int) and m == 0 else sp.snap(18 * m + 6 * g - 12)
                if g == 0:
                    sp.wait_ge(parts_stored, 64 * (m + 1))
                if free_at is not None:
                    sp.wait_ge(b_done, free_at)
                h0 = g * HG * D
                for s0, n, part in QPARTS:
                    for s in range(s0, s0 + n):
                        src = qk_dram[bass.ds(m, 1), 0, part, h0:h0 + HG * D, :].rearrange("o (h d) t -> (o d) h t", h=HG)
                        sp.dma_start(qs[16 * s:16 * s + 16, g, :].rearrange("p (h t) -> p h t", h=HG), src).then_inc(stacks_loaded[g], 16)
                for s0, n in KPARTS:
                    for s in range(s0, s0 + n):
                        src = qk_dram[bass.ds(m, 1), 1, s - s0, h0:h0 + HG * D, :].rearrange("o (h d) t -> (o d) h t", h=HG)
                        sp.dma_start(ks[16 * s:16 * s + 16, g, :].rearrange("p (h t) -> p h t", h=HG), src).then_inc(stacks_loaded[g], 16)
                if g == 0:
                    sp.wait_ge(v_stored, 16 * (m + 1))
                if used_at is not None:
                    sp.wait_ge(pv_done, used_at)
                src = v_dram[bass.ds(m, 1)].rearrange("o p (j c) -> (o p) j c", j=J)[:, :, 128 * g:128 * g + 128]
                sp.dma_start(V[:, g].rearrange("p j h c -> p j (h c)"), src).then_inc(v_loaded[g], 16)

            def load_maxrows(m, g):
                sp.wait_ge(mT_ready, 3 * m + g + 1)
                for c in range(3):
                    dst = qs[KROWS + c:KROWS + c + 1, g, :].rearrange("o (r t) -> o r t", r=TILES)
                    sp.dma_start(dst, mTs[TILES * c:TILES * c + TILES, :]).then_inc(maxrows_loaded[g], 16)

            def store_y(m):
                for n in range(2):
                    sp.wait_ge(y_added, 2 * m + n + 1)
                    dst = out[bass.ds(m, 1)].rearrange("o (p j) e -> (o p) j e", j=J)[:, 3 * n:3 * n + 3, :]
                    sp.dma_start(dst, hB[:, 3 * n:3 * n + 3, :]).then_inc(y_stored, 16)

            def body(b, do_ffn=True, do_pre=True, more=True, nxt=True):
                if do_ffn:
                    load_hA(b)
                load_maxrows(b, 1)
                if nxt:
                    load_stacks(b + 1, 0)
                load_maxrows(b, 2)
                if nxt:
                    load_stacks(b + 1, 1)
                if do_ffn:
                    store_y(b - 1)
                if do_pre and more:
                    load_hP(b + 3)
                if nxt:
                    load_maxrows(b + 1, 0)
                if do_pre:
                    store_parts(b + 2)
                    store_v(b + 2)
                if nxt:
                    load_stacks(b + 1, 2)

            load_hP(1)
            load_hA(0)
            store_parts(0)
            sp.wait_ge(w_split, 4)
            store_v(0)
            for g in range(G3):
                load_stacks(0, g)
            load_hP(2)
            load_maxrows(0, 0)
            store_parts(1)
            store_v(1)
            body(0, do_ffn=False)
            body(1)
            with sp.Fori(2, B - 3) as b:
                body(b)
            body(B - 3, more=False)
            body(B - 2, do_pre=False)
            body(B - 1, do_pre=False, nxt=False)
            store_y(B - 1)
            sp.wait_ge(y_stored, 32 * B)

        @block.gpsimd
        def _(pool):
            def load_w(n):
                _, w, rem = wloads[n]
                for r in range(2):
                    src = w[128:E, :] if rem else w[64 * r:64 * r + 64, :]
                    pool.dma_start(wst[n % 2][64 * r:64 * r + 64, :], src).then_inc(w_loaded[n % 2], 16)

            load_w(0)
            load_w(1)
            nc.gpsimd.memset(neghalf[:], -0.5)
            nc.gpsimd.memset(negone[:], -1.0)
            nc.gpsimd.memset(idle[:], 1.0)
            nc.gpsimd.memset(hn1[:, :, E:E + 1], 1.0)
            nc.gpsimd.memset(vtmp[:], 0.0)
            nc.gpsimd.memset(cw[:], 0.0).then_inc(setup_pool, 1)
            pool.wait_ge(setup_pool, 1)
            nc.gpsimd.memset(vtmp[:, :, :, D:D + 1].rearrange("p j h o -> p (j h) o"), 1.0)
            nc.gpsimd.memset(cw[:, :, NX:NX + 1], 1.0).then_inc(setup_pool, 1)
            for n in range(2, 6):
                pool.wait_ge(w_seen, n - 1)
                load_w(n)
            pool.wait_ge(setup_amax, 1)
            nc.gpsimd.partition_all_reduce(wsc[:, 0:2], wmx[:, 0:2], 128, bass.bass_isa.ReduceOp.max).then_inc(setup_pool, 1)
            P_ = nc.gpsimd
            calls = itertools.count()

            def take_wait():
                k = 1 + next(calls) % 63
                P_.tensor_tensor(idle[:, k:k + 1], idle[:, 0:1], idle[:, 0:1], op=MUL)

            chr_, chw = Chain(pool, ch_route, ROUTE_OPS), Chain(pool, ch_ln1, 1)

            def add_attention(b, g):
                pool.wait_ge(norm_done, 3 * b + g + 1)
                if g == 0:
                    pool.wait_ge(ha_loaded, 16 * (b + 1))
                v = hA[:, :, 64 * g:64 * g + 64]
                P_.tensor_tensor(v, v, onrm[:].rearrange("p (j h) d -> p j (h d)", j=J), op=ADD).then_inc(h_added, 1)

            def ffn_norm(m):
                pool.wait_ge(var2_ready, m + 1)
                P_.tensor_tensor(rstd[:, 1, :], ve[:], neghalf[:], op=ALU.pow).then_inc(pow2_done, 1)
                pool.wait_ge(pow2_done, m + 1)
                P_.tensor_tensor(nmr[:], nmean[:], rstd[:, 1, :], op=MUL).then_inc(rstd2_ready, 1)
                wait(pool, y_stored, 32 * m)
                take_wait()
                P_.tensor_copy(hB, hA).then_inc(hA_free, 1)

            def pre_norm(m):
                pool.wait_ge(var1_ready, m + 1)
                chw.begin(m)
                chw.link(P_.tensor_tensor(rstd[:, 0, :], ve[:], neghalf[:], op=ALU.pow))
                chw.end()
                take_wait()
                for j in range(J):
                    ins = P_.tensor_scalar(hP[:, j, :], hP[:, j, :], mvr[:, j, 0:1], rstd[:, 0, j:j + 1], SUB, MUL)
                ins.then_inc(ln1_ready, 1)

            def third_parts(m):
                for t in range(4):
                    rows = 128 if t % 2 == 0 else E - 128
                    pool.wait_ge(part2_ready, 4 * m + t + 1)
                    P_.tensor_tensor(parts[0:rows, t, 2, :], rest[0:rows, t % 2, :], parts[0:rows, t, 1, :], op=SUB).then_inc(parts_ready, 1)

            def fold(dst, src, n):
                while n > 2:
                    n //= 2
                    chr_.link(P_.tensor_tensor(src[..., 0:n], src[..., 0:n], src[..., n:2 * n], op=ADD))
                chr_.link(P_.tensor_tensor(dst, src[..., 0:1], src[..., 1:2], op=ADD))

            def ranks(s, n, tri, dst):
                L = chr_.link
                c1 = cmp1[:, :, 0:n * n].rearrange("p j (a c) -> p j a c", a=n)
                c2 = cmp2[:, :, 0:n * n].rearrange("p j (a c) -> p j a c", a=n)
                other = s[:, :, None, :].broadcast_to([TP, J, n, n])
                own = s[:, :, :, None].broadcast_to([TP, J, n, n])
                L(P_.tensor_tensor(c2, other, own, op=SUB))
                take_wait()
                L(P_.tensor_scalar(cmp1[:, :, 0:n * n], cmp2[:, :, 0:n * n], 0.0, None, ALU.is_gt))
                take_wait()
                L(P_.tensor_scalar(cmp2[:, :, 0:n * n], cmp2[:, :, 0:n * n], 0.0, None, ALU.is_equal))
                L(P_.tensor_tensor(cmp2[:, :, 0:n * n], cmp2[:, :, 0:n * n], tri[:, None, :].broadcast_to([TP, J, n * n]), op=MUL))
                L(P_.tensor_tensor(cmp1[:, :, 0:n * n], cmp1[:, :, 0:n * n], cmp2[:, :, 0:n * n], op=ADD))
                fold(dst[:, :, :, None], c1, n)

            def route(m):
                L = chr_.link
                chr_.begin(m)
                pool.wait_ge(gexp_ready, m + 1)
                take_wait()
                L(P_.tensor_copy(sbia[:], sc[:]))
                fold(rj[:, 1, :, None], sbia[:], NX)
                L(P_.tensor_tensor(rj[:, 2, :], rj[:, 1, :], negone[:], op=ALU.pow))
                L(P_.tensor_tensor(sc[:], sc[:], rj[:, 2, :, None].broadcast_to([TP, J, NX]), op=MUL))
                L(P_.tensor_tensor(sbia[:], sc[:], gbb[:, None, :].broadcast_to([TP, J, NX]), op=ADD))
                fold(r4[:, 0, :, None], sbia[:].rearrange("p j (q t) -> p (j q) t", t=2), 2)
                ranks(r4[:, 0, :].rearrange("p (j q) -> p j q", j=J), 4, t4, r4[:, 1, :].rearrange("p (j q) -> p j q", j=J))
                take_wait()
                L(P_.tensor_scalar(r4[:, 1, :], r4[:, 1, :], 2.0, None, ALU.is_lt))
                take_wait()
                L(P_.tensor_scalar(r4[:, 2, :], r4[:, 1, :], 3.0e38, -3.0e38, MUL, ADD))
                s24 = sbia[:].rearrange("p j (q t) -> p (j q) t", t=2)
                L(P_.tensor_tensor(s24, s24, r4[:, 1, :, None].broadcast_to([TP, TILES, 2]), op=MUL))
                L(P_.tensor_tensor(s24, s24, r4[:, 2, :, None].broadcast_to([TP, TILES, 2]), op=ADD))
                ranks(sbia[:], NX, t8, rank[:])
                take_wait()
                L(P_.tensor_scalar(rank[:], rank[:], 2.0, None, ALU.is_lt))
                wait(pool, comb_turned, m)
                L(P_.tensor_tensor(cw[:, :, 0:NX], sc[:], rank[:], op=MUL))
                c_ = cw[:, :, 0:NE1]
                take_wait()
                L(P_.tensor_copy(cbf[:], c_))
                take_wait()
                L(P_.tensor_copy(cw[:, :, NE1:2 * NE1], cbf[:]))
                L(P_.tensor_tensor(cres[:], c_, cbf[:], op=SUB))
                take_wait()
                L(P_.tensor_copy(cbf[:], cres[:]))
                take_wait()
                L(P_.tensor_copy(cw[:, :, 2 * NE1:3 * NE1], cbf[:]))
                P_.tensor_tensor(cw[:, :, 3 * NE1:4 * NE1], cres[:], cbf[:], op=SUB).then_inc(comb_ready, 1)
                chr_.end()

            pool.wait_ge(scales_ready, 1)
            ch = Chain(pool, ch_pool, 8)
            for n in range(4, 8):
                which, _, rem = wloads[n]
                hi, lo = (wBh, wBl) if rem else (wAh, wAl)
                w = wst[n % 2]
                pool.wait_ge(w_loaded[n % 2], 32 * (n // 2 + 1))
                if n == 5:
                    pre_norm(0)
                ch.link(nc.gpsimd.tensor_scalar(w, w, wsc[:, 9:10], None, MUL))
                ch.link(nc.gpsimd.tensor_copy(hi[:, which, :], w))
                nc.gpsimd.tensor_tensor(lo[:, which, :], w, hi[:, which, :], op=SUB).then_inc(w_split, 1)
                if n < 6:
                    pool.wait_ge(w_split, n - 3)
                    load_w(n + 2)

            def body(b, do_ffn=True, do_pre=True):
                if do_ffn:
                    add_attention(b - 1, 2)
                    ffn_norm(b - 1)
                    route(b - 1)
                add_attention(b, 0)
                if do_pre:
                    pre_norm(b + 2)
                add_attention(b, 1)
                if do_pre:
                    third_parts(b + 2)

            pre_norm(1)
            third_parts(0)
            third_parts(1)
            body(0, do_ffn=False)
            body(1)
            with pool.Fori(2, B - 2) as b:
                body(b)
            body(B - 2, do_pre=False)
            body(B - 1, do_pre=False)
            add_attention(B - 1, 2)
            ffn_norm(B - 1)
            route(B - 1)

        @block.scalar
        def _(act):
            def halves(t):
                return t.rearrange("p (n c) -> p n c", n=2)

            for dst, src in tok_loads[3:]:
                act.dma_start(dst, src).then_inc(tok_loaded, 16)
            for dst, src in const_loads:
                act.dma_start(dst, src).then_inc(const_loaded, 16)
            act.wait_ge(setup_dve, 1)

            def square(b):
                act.wait_ge(dft_done, b + 1)
                if not isinstance(b, int):
                    act.wait_ge(mel_done, b)
                nc.scalar.activation(halves(power), slot(0, FRAME), ACT.Square).then_inc(power_ready, 1)

            def log(b):
                act.wait_ge(mel_done, b + 1)
                if not isinstance(b, int):
                    act.wait_ge(h0_done, b)
                nc.scalar.activation(halves(logm[0:NMEL, :]), slot(1, NMEL), ACT.Ln, bias=lneps[0:NMEL, :]).then_inc(log_ready, 1)

            square(0)
            log(0)
            with act.Fori(1, B) as b:
                square(b)
                log(b)

            def pre_tile(m, i, s):
                if i < 2:
                    act.wait_ge(x_turned, 2 * m + i + 1)
                    if i == 0:
                        wait(act, proj_done, 7 * m)
                        nc.scalar.activation(halves(xA[:]), slot(s), ACT.Copy).then_inc(xA_ready, 1)
                    else:
                        nc.scalar.activation(halves(xB[0:65, :]), slot(s, 65), ACT.Copy).then_inc(xB_ready, 1)
                elif i < 6:
                    t = i - 2
                    rows = 128 if t % 2 == 0 else E - 128
                    act.wait_ge(proj_done, 7 * m + t + 1)
                    wait(act, parts_ready, 4 * m + t - 1)
                    nc.scalar.activation(halves(rest[0:rows, t % 2, :]), slot(s, rows), ACT.Copy).then_inc(raw_ready, 1)
                    if t == 0:
                        wait(act, parts_stored, 64 * m)
                    act.wait_ge(raw_ready, 4 * m + t + 1)
                    nc.scalar.activation(parts[0:rows, t, 0, :], rest[0:rows, t % 2, :], ACT.Copy).then_inc(part1_ready, 1)
                else:
                    q = i - 6
                    act.wait_ge(proj_done, 7 * m + q + 5)
                    if q == 0:
                        wait(act, v_stored, 16 * m)
                    src = ps[0:TP, 2 * s, 0:2 * E].rearrange("p (j h d) -> p j h d", j=2, h=H)
                    nc.scalar.activation(vtmp[:, 2 * q:2 * q + 2, :, 0:D], src, ACT.Copy).then_inc(v_ready, 1)

            def second_part(m, t):
                rows = 128 if t % 2 == 0 else E - 128
                act.wait_ge(rest_ready, 4 * m + t + 1)
                nc.scalar.activation(parts[0:rows, t, 1, :], rest[0:rows, t % 2, :], ACT.Copy).then_inc(part2_ready, 1)

            def prep_tile(m, i, s):
                act.wait_ge(x2_turned, 2 * m + i + 1)
                raw, hi = ((xA, x2Ah), (xB, x2B))[i]
                if i == 0:
                    wait(act, h3_done, U * m)
                nc.scalar.activation(halves(raw[:]), slot(s), ACT.Copy).then_inc(x2raw_ready, 1)
                act.wait_ge(x2raw_ready, 2 * m + i + 1)
                nc.scalar.activation(hi[:], raw[:], ACT.Copy).then_inc(x2hi_ready, 1)

            def ffn_apply(m, step):
                if step == 0:
                    act.wait_ge(rstd2_ready, m + 1)
                for j in range(3 * step, 3 * step + 3):
                    ins = nc.scalar.activation(hn2[:, j, 0:E], hA[:, j, :], ACT.Identity, bias=nmr[:, j:j + 1], scale=rstd[:, 1, j:j + 1])
                if step == 1:
                    ins.then_inc(ch_dup, 1)
                    act.wait_ge(ch_dup, m + 1)
                    nc.scalar.activation(hn2[:, :, E:256], hn2[:, :, 128:E], ACT.Copy).then_inc(ln2_ready, 1)

            def gate_exp(m):
                act.wait_ge(logits_ready, m + 1)
                nc.scalar.activation(sc[:], lg[:], ACT.Exp).then_inc(gexp_ready, 1)

            def copy_outputs(b, g):
                act.wait_ge(pv_done, 18 * b + 6 * g + 6)
                wait(act, o_turned, 3 * b + g)
                nc.scalar.activation(halves(OT[:]), slot(3), ACT.Copy).then_inc(o_copied, 1)

            def att(b, g, tiles, before=None, hold=False):
                for tile, s in in_slot(tiles):
                    k = tile[1]
                    if ("F", 0) in tiles and tile[0] == "B":
                        if k in (11, 12):
                            ffn_apply(b - 1, k - 11)
                        if k == 21:
                            gate_exp(b - 1)
                    if tile[0] == "P":
                        pre_tile(b + tile[2], k, s)
                        if 3 <= k < 7:
                            second_part(b + tile[2], k - 3)
                    if tile[0] == "F" and k < 2:
                        prep_tile(b - 1, k, s)
                    if tile[0] != "B":
                        continue
                    i, h = k // HG, k % HG
                    act.wait_ge(b_done, 72 * b + 24 * g + k + 1)
                    wait(act, pv_done, 18 * b + 6 * g + i - 1)
                    nc.scalar.activation(halves(probs[:, i % 2, h, :]), slot(s, TP), ACT.Exp).then_inc(exp_done, 1)
                    if k == 1 and before is not None:
                        copy_outputs(*before)
                if not hold:
                    copy_outputs(b, g)

            def ffn(m, outputs=None, turn_at=1):
                for u in range(U):
                    c = u % CH
                    rows = min(128, NFF - 128 * c)
                    act.wait_ge(h1_done, U * m + u + 1)
                    if u >= 2:
                        act.wait_ge(hh_ready, U * m + u - 1)
                    for s in range(2):
                        ins = nc.scalar.activation(h1s[0:rows, u % 2, s, :], ps[0:rows, s, 0:HC], ACT.Identity,
                                                   bias=fb[0:rows, 2, s * CH + c:s * CH + c + 1], scale=wsc[0:rows, 8:9])
                    ins.then_inc(h1_copied, 1)
                    if u == 0 and outputs is not None:
                        copy_outputs(*outputs)
                    if u == turn_at:
                        act.wait_ge(comb_turned, m + 1)
                        wait(act, comb_spread, U * m)
                        nc.scalar.activation(halves(cTb[:]), slot(3, 4 * NE1), ACT.Copy)
                        wait(act, w2_done, U * m)
                        nc.scalar.activation(halves(cT[:]), slot(3, NE1), ACT.Copy).then_inc(combT_ready, 1)
                    act.wait_ge(xg_ready, U * m + u + 1)
                    nc.scalar.activation(th[0:rows, :], xg[0:rows, :], ACT.Tanh, scale=ALPHA / 2).then_inc(tanh_ready, 1)

            def body(b, sections=SECTIONS):
                first, last = isinstance(b, int) and b == 0, isinstance(b, int) and b == B - 1
                att(b, 0, sections[0], None if first else (b - 1, 2), hold=True)
                att(b, 1, sections[1], (b, 0), hold=not first)
                if not first:
                    ffn(b - 1, (b, 1))
                att(b, 2, sections[2], hold=not last)

            for tile, s in in_slot(FIRST):
                if tile[0] == "P":
                    pre_tile(tile[2], tile[1], s)
                    if 3 <= tile[1] < 7:
                        second_part(tile[2], tile[1] - 3)
            body(0, (PLAIN, PLAIN, SECTIONS[2]))
            body(1)
            with act.Fori(2, B - 2) as b:
                body(b)
            body(B - 2, (SECTIONS[0], PLAIN, PLAIN))
            body(B - 1, (SECTIONS[0], schedule(a_tiles=LAST_A), schedule(a_tiles=0)))
            for step in range(2):
                ffn_apply(B - 1, step)
            for i in range(2):
                prep_tile(B - 1, i, i)
            gate_exp(B - 1)
            ffn(B - 1, turn_at=2)

        @block.vector
        def _(dve):
            V_ = nc.vector
            su = Chain(dve, ch_setup, 0)
            V_.memset(logm[32:64, :], 1.0)
            su.link(V_.memset(lneps[:], 1e-6))
            V_.memset(ks[KROWS:KROWS + 32, :, :].rearrange("p g c -> p (g c)"), 1.0)

            def setup_copy(n, dst, rows, cols, scale=1.0):
                dve.wait_ge(setup_pe, n)
                V_.tensor_scalar(dst, ps[0:rows, 7, 0:cols], scale, None, MUL).then_inc(setup_copied, 1)
            setups = [(wc[0:NMEL, :], NMEL, E), (mm_s, D, D, float(D) ** -0.5), (uq2, R, E), (wq[64:65, 1, :], 1, E)]
            for w in (wq, wk, wv):
                setups += [(w[:, 0, :], 128, E), (w[0:64, 1, :], 64, E)]
            dve.wait_ge(tok_loaded, 16 * len(tok_loads))
            V_.tensor_copy(idb[:], idf[:]).then_inc(setup_dve, 1)
            setup_copy(1, *setups[0])

            def largest(k):
                dve.wait_ge(w_loaded[k % 2], 32 * (k // 2 + 1))
                V_.tensor_reduce(wmx[:, 4 + k:5 + k], wst[k % 2], axis=AX.X, op=MAX, apply_absolute_value=True).then_inc(w_seen, 1)

            def largest_all():
                dve.wait_ge(w_seen, 4)
                dve.wait_ge(late_loaded, 16 * len(late_loads))
                V_.tensor_reduce(wmx[:, 0:1], wmx[:, 4:8], axis=AX.X, op=MAX)
                V_.tensor_reduce(wmx[:, 1:2], gstage, axis=AX.X, op=MAX, apply_absolute_value=True).then_inc(setup_amax, 1)

            def scales():
                dve.wait_ge(setup_pool, 3)
                su.link(V_.tensor_scalar(wsc[:, 0:2], wsc[:, 0:2], 1e-30, 1e30, MAX, MIN))
                su.link(V_.tensor_scalar(wsc[:, 3:5].bitcast(i32), wsc[:, 0:2].bitcast(i32), 0x7F800000, None, ALU.bitwise_and))
                su.link(V_.reciprocal(wsc[:, 9:11], wsc[:, 3:5]))
                su.link(V_.tensor_scalar(wsc[:, 9:11], wsc[:, 9:11], 8192.0, None, MUL))
                su.link(V_.tensor_scalar(wsc[:, 6:8], wsc[:, 3:5], 1.0 / (8192.0 * XS), None, MUL))
                V_.reciprocal(wsc[:, 2:3], wsc[:, 6:7])
                su.link(V_.tensor_scalar(wsc[:, 8:9], wsc[:, 6:7], wsc[:, 6:7], None, MUL))
                V_.tensor_scalar(fb[:, 2, :], fb[:, 0, :], wsc[:, 6:7], None, MUL)
                V_.tensor_scalar(fb[:, 3, :], fb[:, 1, :], wsc[:, 2:3], None, MUL).then_inc(scales_ready, 1)
                for half in range(2):
                    s_, h_, l_ = gstage[:, NX * half:NX * half + NX], gwh[:, half, :], gwl[:, half, :]
                    su.link(V_.tensor_scalar(s_, s_, wsc[:, 10:11], None, MUL))
                    su.link(V_.tensor_copy(h_, s_))
                    su.link(V_.tensor_tensor(l_, s_, h_, op=SUB))
                su.link(V_.tensor_copy(selb[:], sel_s))

            def copy_frames(b):
                dve.wait_ge(fr_turned, b + 1)
                wait(dve, dft_done, b)
                V_.tensor_copy(frT.rearrange("p (n c) -> p n c", n=2), slot(0, FRAME)).then_inc(frT_ready, 1)

            def copy_h0(b, q, stored):
                dve.wait_ge(h0_done, b + 1)
                if stored is not None:
                    dve.wait_ge(h0_stored[q], stored)
                V_.tensor_copy(h0t[:, q, :].rearrange("p (n c) -> p n c", n=3), ps[0:TP, 4:7, 0:2 * E]).then_inc(h0_copied, 1)

            chp, cha, chn, chf, chl = (Chain(dve, s, n) for s, n in (
                (ch_pre, 2), (ch_att, 3), (ch_norm, 1), (ch_ffn, 1 + 3 * U), (ch_ln2, 2)))

            def ln_stats(src, j0, n):
                for j in range(j0, j0 + n):
                    ins = V_.bn_stats(st[:, j, :], src[:, j, :])
                return ins

            def ln_var(ch, scale, var_ready):
                V_.memset(ve[:], 0.0)
                for j in range(J):
                    ins = V_.bn_aggr(mvr[:, j, :], st[:, j, :])
                ch.link(ins)
                V_.tensor_scalar(nmean[:], mvr[:, :, 0], -1.0, None, MUL)
                V_.tensor_scalar(ve[:], mvr[:, :, 1], EPS, scale, ADD, MUL).then_inc(var_ready, 1)

            def pre_norm(m, step):
                if step == 0:
                    chp.begin(m)
                    dve.wait_ge(hp_loaded, 16 * (m + 1))
                if step < 3:
                    ins = ln_stats(hP, 2 * step, 2)
                    if step == 2:
                        chp.link(ins)
                if step == 3:
                    ln_var(chp, 1.0, var1_ready)
                    chp.end()

            copy_frames(0)
            for b in range(6):
                copy_frames(b + 1)
                for n in range(3 * b + 1, min(3 * b + 4, len(setups))):
                    setup_copy(n + 1, *setups[n])
                copy_h0(b, b % 2, 16 * (b // 2) if b >= 2 else None)
                if b < 2:
                    largest(2 * b)
                    largest(2 * b + 1)
                if b == 2:
                    largest_all()
                if b == 3:
                    scales()
            for step in range(4):
                pre_norm(0, step)
            with dve.Fori(3, B // 2 - 1) as i:
                for q in range(2):
                    copy_frames(2 * i + q + 1)
                    copy_h0(2 * i + q, q, 16 * i)
            copy_frames(B - 1)
            for q in range(2):
                copy_h0(B - 2 + q, q, 16 * (B // 2 - 1))

            def pre_rest(m, t):
                rows = 128 if t % 2 == 0 else E - 128
                r_ = rest[0:rows, t % 2, :]
                dve.wait_ge(part1_ready, 4 * m + t + 1)
                V_.tensor_tensor(r_, r_, parts[0:rows, t, 0, :], op=SUB).then_inc(rest_ready, 1)

            def amax(a, s, n):
                dve.wait_ge(a_done, a + 1)
                V_.tensor_reduce(negm[:, n:n + 1], slot(s, TP), axis=AX.XY, op=MAX, negate=True).then_inc(max_done, 1)

            def max_parts(G):
                cha.begin(G)
                dve.wait_ge(max_done, 24 * G + 24)
                wait(dve, max_turned, G)
                cha.link(V_.tensor_copy(mpart[:, 0, :], negm[:]))
                cha.link(V_.tensor_tensor(mres[:], negm[:], mpart[:, 0, :], op=SUB))
                cha.link(V_.tensor_copy(mpart[:, 1, :], mres[:]))
                V_.tensor_tensor(mpart[:, 2, :], mres[:], mpart[:, 1, :], op=SUB).then_inc(mparts_ready, 1)
                cha.end()

            def copy_mT(G, s, a, before):
                dve.wait_ge(max_turned, G + 1)
                if a is not None:
                    dve.wait_ge(a_done, a + 1)
                if before is not None:
                    dve.wait_ge(*before)
                V_.tensor_copy(mTs[:], ps[0:3 * TILES, 2 * s + 1, 384:384 + 63].bitcast(bf16)[:, 0:TP]).then_inc(mT_ready, 1)

            def norm(b, g, step):
                G = 3 * b + g
                o4 = ps[0:TP, 6:8, 0:128 * J // 2].rearrange("p n (q c) -> p n q c", q=TILES // 2)
                if step == 0:
                    chn.begin(G)
                    dve.wait_ge(o_turned, G + 1)
                    chn.link(V_.reciprocal(rsum[:].rearrange("p (n q) -> p n q", n=2), o4[:, :, :, D]))
                    wait(dve, h_added, G)
                if step < 2:
                    ins = V_.tensor_tensor(onrm[:, 12 * step:12 * step + 12, :], o4[:, step, :, 0:D],
                                           rsum[:, 12 * step:12 * step + 12, None].broadcast_to([TP, 12, D]), op=MUL)
                    if step == 1:
                        ins.then_inc(norm_done, 1)
                        chn.end()

            def ffn_norm(m, step):
                if step == 0:
                    chl.begin(m)
                    dve.wait_ge(h_added, 3 * m + 3)
                if step < 3:
                    ins = ln_stats(hA, 2 * step, 2)
                    if step == 2:
                        chl.link(ins)
                if step == 3:
                    dve.wait_ge(ln1_ready, min(m + 3, B) if isinstance(m, int) else m + 3)
                    ln_var(chl, XS ** -2, var2_ready)
                    chl.end()

            def ffn_low(m, i):
                dve.wait_ge(x2hi_ready, 2 * m + i + 1)
                if i == 0:
                    V_.tensor_tensor(x2Al[:], xA[:], x2Ah[:], op=SUB).then_inc(x2lo_ready, 1)
                else:
                    V_.tensor_tensor(x2B[64:128, :], xB[64:128, :], x2B[64:128, :], op=SUB).then_inc(x2lo_ready, 1)

            def ffn_logits(m, s):
                chf.begin(m)
                dve.wait_ge(gate_done, m + 1)
                V_.tensor_scalar(lg[:], ps[0:TP, 2 * s, 0:J * NX].rearrange("p (j e) -> p j e", j=J), wsc[0:TP, 7:8], None,
                                 MUL).then_inc(gate_read, 1)
                dve.wait_ge(gate_read, m + 1)
                chf.link(V_.tensor_reduce(rj[:, 0, :], lg[:], axis=AX.X, op=MAX))
                V_.tensor_tensor(lg[:], lg[:], rj[:, 0, :, None].broadcast_to([TP, J, NX]), op=SUB).then_inc(logits_ready, 1)

            def att(b, g, tiles, pre=False):
                before = None if (isinstance(b, int) and b == 0 and g == 0) else (b, g - 1) if g > 0 else (b - 1, 2)
                for tile, s in in_slot(tiles):
                    kind, k = tile[0], tile[1]
                    if k == MT_AT and kind in "AM":
                        copy_mT(3 * b + g + 1, s, 72 * b + 24 * g + k + LEAD if kind == "A" else None,
                                (maxrows_loaded[g], 48 * (b + 1)))
                    if kind == "A":
                        amax(72 * b + 24 * g + k + LEAD, s, (k + LEAD) % TILES)
                        if k == 15:
                            max_parts(3 * b + g + 1)
                    if kind == "F" and k == 2:
                        ffn_logits(b - 1, s)
                    if kind == "B":
                        if before is not None and k == 4:
                            norm(*before, 0)
                            norm(*before, 1)
                        if ("F", 0) in tiles:
                            if 5 <= k < 9:
                                ffn_norm(b - 1, k - 5)
                            if k in (15, 16):
                                ffn_low(b - 1, k - 15)
                        if pre and 6 <= k < 10:
                            pre_norm(b + 2, k - 6)
                        t = PRE_RESTS.get(k)
                        if ("P", 0, 2) in tiles and t is not None:
                            pre_rest(b + 2, t)

            def swiglu(m, u):
                c = u % CH
                rows = min(128, NFF - 128 * c)
                dve.wait_ge(h3_done, U * m + u + 1)
                dve.wait_ge(h1_copied, U * m + u + 1)
                for s in range(2):
                    ins = V_.scalar_tensor_tensor(hh[0:rows, s, :], ps[0:rows, 2 + s, 0:HC], fb[0:rows, 3, s * CH + c:s * CH + c + 1],
                                                  h1s[0:rows, u % 2, s, :], op0=ADD, op1=MUL)
                ins.then_inc(hh_ready, 1)
                dve.wait_ge(hh_ready, U * m + u + 1)
                V_.tensor_scalar(xg[0:rows, :], hh[0:rows, 0, :], LIMIT, None, MIN).then_inc(xg_ready, 1)
                chf.link(V_.tensor_scalar(xl[0:rows, :], hh[0:rows, 1, :], LIMIT, -LIMIT, MIN, MAX))

            def gate_product(m, u):
                c = u % CH
                rows = min(128, NFF - 128 * c)
                dve.wait_ge(xg_ready, U * m + u + 1)
                dve.wait_ge(tanh_ready, U * m + u + 1)
                chf.link(V_.scalar_tensor_tensor(ga[0:rows, :], th[0:rows, :], 1.0, xg[0:rows, :], op0=ADD, op1=MUL))
                chf.link(V_.scalar_tensor_tensor(gt[0:rows, u % 2, :], xl[0:rows, :], 1.0, ga[0:rows, :], op0=ADD, op1=MUL))

            def weigh(m, u):
                c = u % CH
                rows = min(128, NFF - 128 * c)
                dve.wait_ge(comb_spread, U * m + u + 1)
                if u >= 3:
                    dve.wait_ge(w2_done, U * m + u - 2)
                V_.tensor_tensor(gg[0:rows, u % 3, :], ps[0:rows, 4, 0:HC], gt[0:rows, u % 2, :], op=MUL).then_inc(g_ready, 1)

            def add_y(m, n):
                dve.wait_ge(w2_done, U * m + CH * (n + 1))
                dve.wait_ge(hA_free, m + 1)
                v = hB[:, 3 * n:3 * n + 3, :]
                V_.tensor_tensor(v, ps[0:TP, 5:8, 0:E], v, op=ADD).then_inc(y_added, 1)

            def ffn(m):
                for u in range(U):
                    if u == CH + 3:
                        add_y(m, 0)
                    swiglu(m, u)
                    if u >= 2:
                        weigh(m, u - 2)
                    gate_product(m, u)
                weigh(m, U - 2)
                weigh(m, U - 1)
                add_y(m, 1)
                chf.end()

            def body(b, sections=SECTIONS):
                att(b, 0, sections[0])
                att(b, 1, sections[1], pre=("P", 0, 2) in sections[2])
                if not (isinstance(b, int) and b == 0):
                    ffn(b - 1)
                att(b, 2, sections[2])

            for tile, s in in_slot(FIRST):
                kind, k = tile[0], tile[1]
                if kind == "A":
                    n = k + LEAD
                    if n == TILES + 2:
                        copy_mT(0, s, n, None)
                    amax(n, s, n % TILES)
                    if n == TILES - 1:
                        max_parts(0)
                if kind == "P" and 3 <= k < 7:
                    pre_rest(tile[2], k - 3)
                if kind == "P" and k == 2 and tile[2] == 0:
                    for step in range(4):
                        pre_norm(1, step)
            body(0, (PLAIN, PLAIN, SECTIONS[2]))
            body(1)
            with dve.Fori(2, B - 2) as b:
                body(b)
            body(B - 2, (SECTIONS[0], PLAIN, PLAIN))
            body(B - 1, (SECTIONS[0], schedule(a_tiles=LAST_A), schedule(a_tiles=0)))
            for step in range(2):
                norm(B - 1, 2, step)
            for step in range(4):
                ffn_norm(B - 1, step)
            ffn_low(B - 1, 0)
            ffn_low(B - 1, 1)
            ffn_logits(B - 1, 2)
            ffn(B - 1)

        @block.tensor
        def _(pe):
            def mm(o, l, r, start=True, stop=True):
                return nc.tensor.matmul(o, l, r, start=start, stop=stop)

            def b7(rows, c0, c1):
                return ps[0:rows, 7, c0:c1]
            pe.wait_ge(tok_loaded, 16 * len(tok_loads))
            mm(b7(NMEL, 0, E), dct_s, wp_s).then_inc(setup_pe, 1)

            def setup_product(n):
                if n == 2:
                    pe.wait_ge(const_loaded, 16 * len(const_loads))
                pe.wait_ge(setup_copied, n - 1)
                if n == 2:
                    ins = mm(b7(D, 0, D), muT_s, mv_s)
                elif n == 3:
                    for h in range(H):
                        ins = mm(b7(R, D * h, D * h + D), uqh_s[:, R * h:R * h + R], mm_s)
                elif n == 4:
                    for h in range(H):
                        ins = mm(b7(1, D * h, D * h + D), bqh_s[:, h:h + 1], mm_s)
                else:
                    l, r_ = ((vqT_s, uq2), (vkT_s, uk_s), (vvT_s, uv_s))[(n - 5) // 2]
                    ins = mm(b7(128, 0, E), l[:, 0:128], r_) if n % 2 == 1 else mm(b7(64, 0, E), l[:, 128:E], r_)
                ins.then_inc(setup_pe, 1)

            pe.wait_ge(setup_dve, 1)

            def halves(s, rows, l, r):
                for q in range(2):
                    ins = mm(slot(s, rows)[:, q, :], l, r[:, HC * q:HC * q + HC])
                return ins

            def turn_frames(b, q, loaded):
                pe.wait_ge(fr_loaded[q], loaded)
                if not (isinstance(b, int) and b == 0):
                    pe.wait_ge(power_ready, b)
                for j in range(J):
                    ins = nc.tensor.transpose(ps[0:FRAME, j // 3, TP * (j % 3):TP * (j % 3) + TP], frames[:, q, j, :], idf[0:TP, 0:TP])
                ins.then_inc(fr_turned, 1)

            def transform(b):
                pe.wait_ge(frT_ready, b + 1)
                halves(0, FRAME, dfts[:], frT).then_inc(dft_done, 1)

            def energies(b):
                pe.wait_ge(power_ready, b + 1)
                if not (isinstance(b, int) and b == 0):
                    pe.wait_ge(log_ready, b)
                halves(1, NMEL, melS[:], power).then_inc(mel_done, 1)

            def project(b):
                pe.wait_ge(log_ready, b + 1)
                if not (isinstance(b, int) and b == 0):
                    pe.wait_ge(h0_copied, b)
                for j in range(J):
                    ins = mm(ps[0:TP, 4 + j // 2, E * (j % 2):E * (j % 2) + E], logm[0:NMEL + 1, TP * j:TP * j + TP], wc[0:NMEL + 1, :])
                ins.then_inc(h0_done, 1)

            def token_step(b, q, loaded, setup=(None, None, None)):
                turn_frames(b + 1, q, loaded)
                if setup[0]:
                    setup_product(setup[0])
                energies(b)
                if setup[1]:
                    setup_product(setup[1])
                transform(b + 1)
                if setup[2]:
                    setup_product(setup[2])
                project(b)

            turn_frames(0, 0, 16)
            transform(0)
            for b in range(3):
                token_step(b, b + 1, 16, (3 * b + 2, 3 * b + 3, 3 * b + 4))
            with pe.Fori(1, B // 4) as i:
                for q in range(4):
                    token_step(4 * i + q - 1, q, 16 * i + 16)
            energies(B - 1)
            project(B - 1)
            pe.wait_ge(h0_copied, B)
            pe.wait_ge(setup_copied, 10)

            def turn(src, c0, cols, s):
                for j in range(J):
                    ins = nc.tensor.transpose(ps[0:cols, 2 * s + j // 3, TP * (j % 3):TP * (j % 3) + TP], src[:, j, c0:c0 + cols], idf[0:TP, 0:TP])
                return ins

            def pre_tile(m, i, s):
                if i < 2:
                    if i == 0:
                        pe.wait_ge(ln1_ready, m + 1)
                    turn(hn1, 128 * i, (128, 65)[i], s).then_inc(x_turned, 1)
                elif i < 6:
                    w = (wq, wk)[(i - 2) // 2]
                    f0, rows = (0, 128) if i % 2 == 0 else (128, E - 128)
                    if i == 2:
                        pe.wait_ge(xA_ready, m + 1)
                        pe.wait_ge(xB_ready, m + 1)
                    for q in range(2):
                        mm(slot(s, rows)[:, q, :], w[:, 0, f0:f0 + rows], xA[:, HC * q:HC * q + HC], True, False)
                        ins = mm(slot(s, rows)[:, q, :], w[0:65, 1, f0:f0 + rows], xB[0:65, HC * q:HC * q + HC], False, True)
                    ins.then_inc(proj_done, 1)
                else:
                    for j in (2 * i - 12, 2 * i - 11):
                        o = ps[0:TP, 2 * s, E * (j % 2):E * (j % 2) + E]
                        mm(o, xA[:, TP * j:TP * j + TP], wv[:, 0, :], True, False)
                        ins = mm(o, xB[0:65, TP * j:TP * j + TP], wv[0:65, 1, :], False, True)
                    ins.then_inc(proj_done, 1)

            def prep_tile(m, i, s):
                if i < 2:
                    if i == 0:
                        pe.wait_ge(ln2_ready, m + 1)
                    turn(hn2, 128 * i, 128, s).then_inc(x2_turned, 1)
                else:
                    pe.wait_ge(x2hi_ready, 2 * m + 2)
                    pe.wait_ge(x2lo_ready, 2 * m + 2)
                    for j in range(J):
                        c = slice(TP * j, TP * j + TP)
                        o = ps[0:TP, 2 * s, NX * j:NX * j + NX]
                        mm(o, x2Ah[:, c], gwh[:, 0, :], True, False)
                        mm(o, x2Ah[:, c], gwl[:, 0, :], False, False)
                        mm(o, x2Al[:, c], gwh[:, 0, :], False, False)
                        mm(o, x2B[:, c], gwh[:, 1, :], False, False)
                        ins = mm(o, x2B[:, c], gwl[:, 1, :], False, True)
                    ins.then_inc(gate_done, 1)

            def a_tile(g, n, s):
                h, j = n // J, n % J
                for q in range(2):
                    ins = mm(slot(s, TP)[:, q, :], qs[0:KROWS, g, NF * h + TP * j:NF * h + TP * j + TP],
                             ks[0:KROWS, g, NF * h + HC * q:NF * h + HC * q + HC])
                ins.then_inc(a_done, 1)

            def b_tile(g, k, s):
                i, h = k // HG, k % HG
                K = KROWS + MROWS
                for q in range(2):
                    ins = mm(slot(s, TP)[:, q, :], ks[0:K, g, NF * h + TP * i:NF * h + TP * i + TP],
                             qs[0:K, g, NF * h + HC * q:NF * h + HC * q + HC])
                ins.then_inc(b_done, 1)

            def turn_maxima(G, s):
                pe.wait_ge(mparts_ready, G + 1)
                nc.tensor.transpose(ps[0:3 * TILES, 2 * s + 1, 384:384 + 63].bitcast(bf16)[:, 0:TP],
                                    mpart[:].rearrange("p c r -> p (c r)"), idb[0:TP, 0:TP]).then_inc(max_turned, 1)

            def pv(b, g, i, part):
                if part == 0:
                    pe.wait_ge(exp_done, 72 * b + 24 * g + 4 * i + 4)
                    if i == 0:
                        wait(pe, norm_done, 3 * b + g)
                        pe.wait_ge(v_loaded[g], 16 * (b + 1))
                c0, c1 = PV_COLS[part]
                q = c0 // HC
                for h in range(HG):
                    ins = mm(ps[32 * h:32 * h + 32, 6 + q, c0 - HC * q:c1 - HC * q], V[:, g, i, h, :], probs[:, i % 2, h, c0:c1],
                             i == 0 and c0 % HC == 0, i == J - 1 and c1 % HC == 0)
                if part == len(PV_COLS) - 1:
                    ins.then_inc(pv_done, 1)

            def turn_outputs(G):
                pe.wait_ge(o_copied, G + 1)
                for j in range(J):
                    ins = nc.tensor.transpose(ps[0:TP, 6 + j // 3, 128 * (j % 3):128 * (j % 3) + 128], OT[:, TP * j:TP * j + TP], idf[:])
                ins.then_inc(o_turned, 1)

            def slot_read(tiles, p, b, g, before):
                while p >= 3:
                    p -= 3
                    if tiles[p] is not None:
                        return wait(pe, *tile_read(tiles[p], b, g))
                if before is not None:
                    tiles, b, g = before
                    return slot_read(tiles, len(tiles) + p, b, g, None)

            def pv_parts(b, g, parts):
                for n in parts:
                    pv(b, g, n // len(PV_COLS), n % len(PV_COLS))

            def att(b, g, tiles, before, tail=None, pending=None, hold=False):
                first = isinstance(b, int) and b == 0 and g == 0
                for p, tile in enumerate(tiles):
                    if tile is None:
                        continue
                    kind, k, s = tile[0], tile[1], p % 3
                    slot_read(tiles, p, b, g, before)
                    if k == MT_AT and kind in "AM":
                        turn_maxima(3 * b + g + 1, s)
                    if kind == "A":
                        gn, n = (g + 1 + (k + 8) // TILES) % 3, (k + LEAD) % TILES
                        if n == 0:
                            pe.wait_ge(stacks_loaded[gn], 192 * (b + 1 + (1 if g + 2 > 2 else 0)))
                        a_tile(gn, n, s)
                    if kind == "P":
                        pre_tile(b + tile[2], k, s)
                    if kind == "F":
                        prep_tile(b - 1, k, s)
                    if kind == "B":
                        if k == 0:
                            pe.wait_ge(maxrows_loaded[g], 48 * (b + 1))
                        b_tile(g, k, s)
                        if k == TURN_O and not first:
                            turn_outputs(3 * b + g - 1)
                    if pending is not None and kind in "AB" and k < 2:
                        if ("A", k) in tiles:
                            pv_parts(*pending, (PV_LAST[2 * k + (kind == "B")],))
                        elif kind == "B":
                            pv_parts(*pending, PV_LAST[2 * k:2 * k + 2])
                    if kind == ("A" if ("A", k) in tiles else "B") and k > PV_FROM:
                        if k == PV_FROM + 1:
                            pv_parts(b, g, (0,))
                        pv_parts(b, g, (k - PV_FROM,))
                    if tail is not None and k == 0 and kind in "AB":
                        if ("A", 0) not in tiles:
                            ffn_tail(tail, 0)
                        ffn_tail(tail, 0 if kind == "A" else 1)
                pv_parts(b, g, range(TILES - PV_FROM, PV_LAST[0]))
                if not hold:
                    pv_parts(b, g, PV_LAST)

            def first_product(m, u, which, s):
                n, c = u // CH, u % CH
                rows = min(128, NFF - 128 * c)
                t = slice(HC * n, HC * n + HC)
                for q in range(2):
                    f = slice(NFF * q + 128 * c, NFF * q + 128 * c + rows)
                    o = slot(s, rows)[:, q, :]
                    mm(o, wAh[:, which, f], x2Ah[:, t], True, False)
                    mm(o, wAl[:, which, f], x2Ah[:, t], False, False)
                    mm(o, wAh[:, which, f], x2Al[:, t], False, False)
                    mm(o, wBh[:, which, f], x2B[:, t], False, False)
                    ins = mm(o, wBl[:, which, f], x2B[:, t], False, True)
                return ins

            def spread(m, u):
                n, c = u // CH, u % CH
                rows = min(128, NFF - 128 * c)
                if u == 0:
                    pe.wait_ge(combT_ready, m + 1)
                else:
                    pe.wait_ge(g_ready, U * m + u)
                mm(ps[0:rows, 4, 0:HC], selb[:, 128 * c:128 * c + rows], cTb[:, HC * n:HC * n + HC]).then_inc(comb_spread, 1)

            def second_product(m, u):
                n, c = u // CH, u % CH
                rows = min(128, NFF - 128 * c)
                if c == 0:
                    if n == 1:
                        pe.wait_ge(y_added, 2 * m + 1)
                    for jj in range(3):
                        t = slice(HC * n + TP * jj, HC * n + TP * jj + TP)
                        mm(ps[0:TP, 5 + jj, 0:E], cT[:, t], b2s[:], True, False)
                pe.wait_ge(g_ready, U * m + u + 1)
                for jj in range(3):
                    ins = mm(ps[0:TP, 5 + jj, 0:E], gg[0:rows, u % 3, TP * jj:TP * jj + TP], w2s[0:rows, c, :], False, c == CH - 1)
                ins.then_inc(w2_done, 1)

            def ffn(m, before=None, turn_at=1):
                for u in range(U):
                    if u > 0:
                        pe.wait_ge(h1_copied, U * m + u)
                    elif before is not None:
                        slot_read(before[0], len(before[0]), before[1], before[2], None)
                    first_product(m, u, 0, 0).then_inc(h1_done, 1)
                    if u == 0 and before is not None:
                        slot_read(before[0], len(before[0]) + 1, before[1], before[2], None)
                    if u == 1 and before is not None:
                        pe.wait_ge(o_copied, 3 * before[1] + before[2] + 1)
                    if u == turn_at:
                        pe.wait_ge(comb_ready, m + 1)
                        for j in range(J):
                            ins = nc.tensor.transpose(ps[0:72, 6 + j // 3, TP * (j % 3):TP * (j % 3) + TP], cw[:, j, :], idf[0:TP, 0:TP])
                        ins.then_inc(comb_turned, 1)
                    if u > 0:
                        pe.wait_ge(hh_ready, U * m + u)
                    first_product(m, u, 1, 1).then_inc(h3_done, 1)
                    if u == 0 and before is not None:
                        pv_parts(before[1], before[2], PV_LAST)
                    if u >= 2:
                        spread(m, u - 2)
                    if u >= 3:
                        second_product(m, u - 3)

            def ffn_tail(m, step):
                if step == 0:
                    spread(m, U - 2)
                    second_product(m, U - 3)
                else:
                    spread(m, U - 1)
                    second_product(m, U - 2)
                    second_product(m, U - 1)
                    pe.wait_ge(y_added, 2 * m + 2)

            def body(b, sections=SECTIONS, before=None):
                before0 = before if before is not None else (SECTIONS[2], b - 1, 2)
                first, last = isinstance(b, int) and b == 0, isinstance(b, int) and b == B - 1
                att(b, 0, sections[0], before0, pending=None if first else (b - 1, 2), hold=True)
                att(b, 1, sections[1], (sections[0], b, 0), pending=(b, 0), hold=not first)
                if first:
                    att(b, 2, sections[2], (sections[1], b, 1), hold=True)
                else:
                    ffn(b - 1, (sections[1], b, 1))
                    pe.wait_ge(h1_copied, U * b)
                    pe.wait_ge(hh_ready, U * b)
                    att(b, 2, sections[2], None, tail=b - 1, hold=not last)

            for p, tile in enumerate(FIRST):
                if tile is None:
                    continue
                slot_read(FIRST, p, 0, 0, None)
                if tile[0] == "P":
                    pre_tile(tile[2], tile[1], p % 3)
                else:
                    n = tile[1] + LEAD
                    if n % TILES == 0:
                        pe.wait_ge(stacks_loaded[n // TILES], 192)
                    if n == TILES + 2:
                        turn_maxima(0, p % 3)
                    a_tile(n // TILES, n % TILES, p % 3)
            body(0, (PLAIN, PLAIN, SECTIONS[2]), (FIRST, 0, 0))
            body(1)
            with pe.Fori(2, B - 2) as b:
                body(b)
            body(B - 2, (SECTIONS[0], PLAIN, PLAIN))
            body(B - 1, (SECTIONS[0], schedule(a_tiles=LAST_A), schedule(a_tiles=0)), (PLAIN, B - 2, 2))
            pe.wait_ge(exp_done, NPAIR)
            turn_outputs(3 * B - 1)
            pe.wait_ge(norm_done, 3 * B)
            for i in range(NPREP):
                prep_tile(B - 1, i, i)
            ffn(B - 1, turn_at=2)
            ffn_tail(B - 1, 0)
            ffn_tail(B - 1, 1)


ROUTE_OPS = 34


def kernel(**inputs):
    import numpy as np
    import concourse.bacc as bacc
    from concourse.bass_utils import run_bass_kernel_spmd

    def a(name):
        return np.asarray(inputs[name])

    def both(per_expert, shared):
        cols = []
        for s in range(2):
            p = per_expert[:, :, s::2]
            cols += [p.transpose(1, 0, 2).reshape(p.shape[1], NX * I), shared[:, s::2]]
        return np.concatenate(cols, axis=1)

    def by_chunk(bias):
        z = np.zeros((2, CH * 128), bias.dtype)
        z[:, 0:NFF] = bias.reshape(2, NFF)
        return z.reshape(2 * CH, 128).T

    s = np.arange(FRAME)
    window = 0.54 - 0.46 * np.cos(2.0 * np.pi * s / (FRAME - 1))
    k = np.arange(BINS)
    angle = 2.0 * np.pi * np.outer(s, k) / FRAME
    dft = (window[:, None] * np.concatenate([np.cos(angle), np.sin(angle[:, 1:BINS - 1])], axis=1)).astype(np.float32)
    sel = np.zeros((4 * NE1, CH * 128), np.float32)
    for c in range(3):
        for f in range(NFF):
            sel[NE1 * (c + 1) + f // I, f] = 0.5

    p = "L0_attn_"
    f = "L0_ffn_"
    arrays = dict(
        x=a("x"), melT=a("L0_tok_mel_filters").T, dct=a("L0_tok_dct"), w_proj=a("L0_tok_w_proj"), b_proj=a("L0_tok_b_proj")[None],
        vqT=a(p + "V_Q").T, uqh=a(p + "U_Q").reshape(R, H, D).transpose(2, 1, 0).reshape(D, H * R),
        vkT=a(p + "V_K").T, uk=a(p + "U_K"), vvT=a(p + "V_V").T, uv=a(p + "U_V"),
        bqh=a(p + "bias_q").reshape(H, D).T, bk=a(p + "bias_k")[None], bv=a(p + "bias_v")[None],
        muT=a(p + "M_U").T, mv=a(p + "M_V"), gwT=a(f + "gate_w").T, gb=a(f + "gate_b")[None],
        w1=both(a(f + "W1"), a(f + "Ws1")), b1=by_chunk(both(a(f + "B1")[:, None, :], a(f + "Bs1")[None])),
        w3=both(a(f + "W3"), a(f + "Ws3")), b3=by_chunk(both(a(f + "B3")[:, None, :], a(f + "Bs3")[None])),
        w2=np.concatenate([a(f + "W2").reshape(NX * I, E), a(f + "Ws2")]), b2=np.concatenate([a(f + "B2"), a(f + "Bs2")[None]]),
        dft=dft, ident=np.eye(128, dtype=np.float32),
        tri4=np.tri(4, 4, -1, dtype=np.float32).reshape(1, 16), tri8=np.tri(8, 8, -1, dtype=np.float32).reshape(1, 64), sel=sel,
    )
    nc = bacc.Bacc("TRN2", target_bir_lowering=False, num_devices=1)
    fed, aps = {}, {}
    for name, v in arrays.items():
        v = np.ascontiguousarray(v)
        fed["in_" + name] = v
        aps[name] = nc.dram_tensor("in_" + name, v.shape, mybir.dt.from_np(v.dtype), kind="ExternalInput").ap()
    aps["out"] = nc.dram_tensor("out", (B, NF, E), mybir.dt.float32, kind="ExternalOutput").ap()
    build(nc, **aps)
    return run_bass_kernel_spmd(nc, [fed], core_ids=[0]).results[0]["out"]
```
